# Optimizing a Trainium2 kernel written in Bass

```python
import numpy as np
import jax
import jax.numpy as jnp

def _softmax(x, axis=-1):
    return jax.nn.softmax(x, axis=axis)

def _gelu(x):
    return jax.nn.gelu(x, approximate=True)

def _silu(x):
    return jax.nn.silu(x)

def _sigmoid(x):
    return jax.nn.sigmoid(x)

def _layernorm(x, axis=-1, eps=1e-05):
    m = jnp.mean(x, axis=axis, keepdims=True)
    v = jnp.var(x, axis=axis, keepdims=True)
    return (x - m) / jnp.sqrt(v + eps)

def _scatter_add(tgt, idx, src, axis=0):
    return tgt.at[idx].add(src)

def _segment_sum(src, seg, n):
    return jax.ops.segment_sum(src, seg, n)
kernel_name = 'mk_seq_postln_d2_jaxref_r8_919155'

def setup_inputs(seed: int=0):
    np.random.seed(seed)
    _w = jnp.asarray

    def _L0_attn_setup():
        import jax, jax.numpy as jnp
        import numpy as np
        import math
        EMBED_DIM = 128
        NUM_HEADS = 16
        HEAD_DIM = EMBED_DIM // NUM_HEADS
        BLOCK = 64
        SCALE = 1.0 / math.sqrt(HEAD_DIM)

        def _flash_attn(Q, K, V):
            B, H, S, hd = Q.shape
            nkb = S // BLOCK
            Kb = K.reshape(B, H, nkb, BLOCK, hd).transpose(2, 0, 1, 3, 4)
            Vb = V.reshape(B, H, nkb, BLOCK, hd).transpose(2, 0, 1, 3, 4)
            out0 = jnp.zeros_like(Q)
            m0 = jnp.full((B, H, S, 1), -jnp.inf, dtype=Q.dtype)
            l0 = jnp.zeros((B, H, S, 1), dtype=Q.dtype)

            def body(carry, kv):
                out, m, l = carry
                K_blk, V_blk = kv
                scores = jnp.einsum('bhqd,bhkd->bhqk', Q, K_blk) * SCALE
                M_ij = scores.max(axis=-1, keepdims=True)
                m_new = jnp.maximum(m, M_ij)
                corr = jnp.exp(m - m_new)
                exp_scores = jnp.exp(scores - m_new)
                chunk_sum = exp_scores.sum(axis=-1, keepdims=True)
                l_new = chunk_sum * corr + chunk_sum
                out_new = out * corr + jnp.einsum('bhqk,bhkd->bhqd', exp_scores, V_blk)
                return ((out_new, m_new, l_new), None)
            (out, m, l), _ = jax.lax.scan(body, (out0, m0, l0), (Kb, Vb))
            return out / l
        key = jax.random.key(seed)
        ks = jax.random.split(key, 6)
        B, S, E = (4, 256, EMBED_DIM)
        std = 1.0 / math.sqrt(E)
        return {'x': jax.random.normal(ks[0], (B, S, E), dtype=jnp.float32), 'q_w': jax.random.normal(ks[1], (E, E), dtype=jnp.float32) * std, 'k_w': jax.random.normal(ks[2], (E, E), dtype=jnp.float32) * std, 'v_w': jax.random.normal(ks[3], (E, E), dtype=jnp.float32) * std, 'out_w': jax.random.normal(ks[4], (E, E), dtype=jnp.float32) * std, 'out_b': jnp.zeros((E,), dtype=jnp.float32)}
    _L0_attn_in = _L0_attn_setup()

    def _L0_ffn_setup():
        import jax, jax.numpy as jnp
        import numpy as np
        D_IN, D_HID = (128, 512)

        def _ternary(key, shape):
            return jax.random.randint(key, shape, -1, 2).astype(jnp.float32)

        def _tlin(x, w, s):
            return jnp.einsum('bsi,oi->bso', x, w) * s
        key = jax.random.key(seed)
        ks = jax.random.split(key, 12)
        inv = lambda fan: 1.0 / np.sqrt(fan).astype(np.float32)
        return {'x': jax.random.normal(ks[0], (4, 256, D_IN), dtype=jnp.float32), 'w1_w': _ternary(ks[1], (D_HID, D_IN)), 'w1_s': jax.random.uniform(ks[2], (D_HID,), dtype=jnp.float32) * inv(D_IN), 'w2_w': _ternary(ks[3], (D_HID, D_IN)), 'w2_s': jax.random.uniform(ks[4], (D_HID,), dtype=jnp.float32) * inv(D_IN), 'h1_w': _ternary(ks[5], (D_HID, D_HID)), 'h1_s': jax.random.uniform(ks[6], (D_HID,), dtype=jnp.float32) * inv(D_HID), 'h2_w': _ternary(ks[7], (D_HID, D_HID)), 'h2_s': jax.random.uniform(ks[8], (D_HID,), dtype=jnp.float32) * inv(D_HID), 'w3_w': _ternary(ks[9], (D_IN, D_HID)), 'w3_s': jax.random.uniform(ks[10], (D_IN,), dtype=jnp.float32) * inv(D_HID)}
    _L0_ffn_in = _L0_ffn_setup()

    def _L1_attn_setup():
        import jax, jax.numpy as jnp
        import numpy as np
        D_MODEL = 128
        SCALE = float(np.sqrt(D_MODEL))
        key = jax.random.key(seed)
        k1, k2, k3 = jax.random.split(key, 3)
        input_data = jax.random.normal(k1, (4, 256, D_MODEL), dtype=jnp.float32)
        qk = jax.random.normal(k2, (D_MODEL, D_MODEL), dtype=jnp.float32) / SCALE
        ov = jax.random.normal(k3, (D_MODEL, D_MODEL), dtype=jnp.float32) / SCALE
        return {'input_data': input_data, 'qk': qk, 'ov': ov}
    _L1_attn_in = _L1_attn_setup()

    def _L1_ffn_setup():
        import jax, jax.numpy as jnp
        import numpy as np
        LN_EPS = 1e-05
        NORM_EPS = 1e-12

        def _layernorm(x, gamma, beta):
            mu = x.mean(axis=-1, keepdims=True)
            var = ((x - mu) ** 2).mean(axis=-1, keepdims=True)
            return (x - mu) * jax.lax.rsqrt(var + LN_EPS) * gamma + beta

        def _l2norm(x, axis):
            n = jnp.sqrt((x ** 2).sum(axis=axis, keepdims=True))
            return x / jnp.maximum(n, NORM_EPS)
        key = jax.random.key(seed)
        ks = jax.random.split(key, 4)
        B, N, D, E, S, H = (64, 32, 128, 16, 16, 32)
        x = jax.random.normal(ks[0], (B, N, D), dtype=jnp.float32)
        mu = jax.random.normal(ks[1], (D, E, S), dtype=jnp.float32) / np.sqrt(D)
        w1 = jax.random.normal(ks[2], (E, D, H), dtype=jnp.float32) * np.sqrt(2.0 / D)
        w2 = jax.random.normal(ks[3], (E, H, D), dtype=jnp.float32) * np.sqrt(2.0 / (H + D))
        return {'x': x, 'ln_gamma': jnp.ones((D,), jnp.float32), 'ln_beta': jnp.zeros((D,), jnp.float32), 'mu': mu, 'scale': jnp.ones((1,), jnp.float32), 'w1': w1, 'b1': jnp.zeros((E, H), jnp.float32), 'w2': w2, 'b2': jnp.zeros((E, D), jnp.float32)}
    _L1_ffn_in = _L1_ffn_setup()
    _d = {'L0_attn_x': _L0_attn_in['x'], 'L0_attn_q_w': _L0_attn_in['q_w'], 'L0_attn_k_w': _L0_attn_in['k_w'], 'L0_attn_v_w': _L0_attn_in['v_w'], 'L0_attn_out_w': _L0_attn_in['out_w'], 'L0_attn_out_b': _L0_attn_in['out_b'], 'L0_ffn_w1_w': _L0_ffn_in['w1_w'], 'L0_ffn_w1_s': _L0_ffn_in['w1_s'], 'L0_ffn_w2_w': _L0_ffn_in['w2_w'], 'L0_ffn_w2_s': _L0_ffn_in['w2_s'], 'L0_ffn_h1_w': _L0_ffn_in['h1_w'], 'L0_ffn_h1_s': _L0_ffn_in['h1_s'], 'L0_ffn_h2_w': _L0_ffn_in['h2_w'], 'L0_ffn_h2_s': _L0_ffn_in['h2_s'], 'L0_ffn_w3_w': _L0_ffn_in['w3_w'], 'L0_ffn_w3_s': _L0_ffn_in['w3_s'], 'L1_attn_qk': _L1_attn_in['qk'], 'L1_attn_ov': _L1_attn_in['ov'], 'L1_ffn_ln_gamma': _L1_ffn_in['ln_gamma'], 'L1_ffn_ln_beta': _L1_ffn_in['ln_beta'], 'L1_ffn_mu': _L1_ffn_in['mu'], 'L1_ffn_scale': _L1_ffn_in['scale'], 'L1_ffn_w1': _L1_ffn_in['w1'], 'L1_ffn_b1': _L1_ffn_in['b1'], 'L1_ffn_w2': _L1_ffn_in['w2'], 'L1_ffn_b2': _L1_ffn_in['b2']}
    _x0 = _d['L0_attn_x']
    _d['L0_attn_x'] = jax.random.normal(jax.random.fold_in(jax.random.key(seed), 1), (8, 1024, 128), dtype=_x0.dtype)
    del _x0
    return _d

def reference(L0_attn_x, L0_attn_q_w, L0_attn_k_w, L0_attn_v_w, L0_attn_out_w, L0_attn_out_b, L0_ffn_w1_w, L0_ffn_w1_s, L0_ffn_w2_w, L0_ffn_w2_s, L0_ffn_h1_w, L0_ffn_h1_s, L0_ffn_h2_w, L0_ffn_h2_s, L0_ffn_w3_w, L0_ffn_w3_s, L1_attn_qk, L1_attn_ov, L1_ffn_ln_gamma, L1_ffn_ln_beta, L1_ffn_mu, L1_ffn_scale, L1_ffn_w1, L1_ffn_b1, L1_ffn_w2, L1_ffn_b2):

    def _L0_attn_ref(x, q_w, k_w, v_w, out_w, out_b):
        import jax, jax.numpy as jnp
        import numpy as np
        import math
        EMBED_DIM = 128
        NUM_HEADS = 16
        HEAD_DIM = EMBED_DIM // NUM_HEADS
        BLOCK = 64
        SCALE = 1.0 / math.sqrt(HEAD_DIM)

        def _flash_attn(Q, K, V):
            B, H, S, hd = Q.shape
            nkb = S // BLOCK
            Kb = K.reshape(B, H, nkb, BLOCK, hd).transpose(2, 0, 1, 3, 4)
            Vb = V.reshape(B, H, nkb, BLOCK, hd).transpose(2, 0, 1, 3, 4)
            out0 = jnp.zeros_like(Q)
            m0 = jnp.full((B, H, S, 1), -jnp.inf, dtype=Q.dtype)
            l0 = jnp.zeros((B, H, S, 1), dtype=Q.dtype)

            def body(carry, kv):
                out, m, l = carry
                K_blk, V_blk = kv
                scores = jnp.einsum('bhqd,bhkd->bhqk', Q, K_blk) * SCALE
                M_ij = scores.max(axis=-1, keepdims=True)
                m_new = jnp.maximum(m, M_ij)
                corr = jnp.exp(m - m_new)
                exp_scores = jnp.exp(scores - m_new)
                chunk_sum = exp_scores.sum(axis=-1, keepdims=True)
                l_new = chunk_sum * corr + chunk_sum
                out_new = out * corr + jnp.einsum('bhqk,bhkd->bhqd', exp_scores, V_blk)
                return ((out_new, m_new, l_new), None)
            (out, m, l), _ = jax.lax.scan(body, (out0, m0, l0), (Kb, Vb))
            return out / l
        B, S, E = x.shape
        H, hd = (NUM_HEADS, HEAD_DIM)

        def split_heads(t):
            return t.reshape(B, S, H, hd).transpose(0, 2, 1, 3)
        Q = split_heads(x @ q_w.T)
        K = split_heads(x @ k_w.T)
        V = split_heads(x @ v_w.T)
        out = _flash_attn(Q, K, V)
        out = out.transpose(0, 2, 1, 3).reshape(B, S, E)
        return out @ out_w.T + out_b

    def _L0_ffn_ref(x, w1_w, w1_s, w2_w, w2_s, h1_w, h1_s, h2_w, h2_s, w3_w, w3_s):
        import jax, jax.numpy as jnp
        import numpy as np
        D_IN, D_HID = (128, 512)

        def _ternary(key, shape):
            return jax.random.randint(key, shape, -1, 2).astype(jnp.float32)

        def _tlin(x, w, s):
            return jnp.einsum('bsi,oi->bso', x, w) * s
        h = jax.nn.silu(_tlin(x, w1_w, w1_s)) * _tlin(x, w2_w, w2_s)
        h = jax.nn.gelu(_tlin(h, h1_w, h1_s), approximate=False)
        h = jax.nn.gelu(_tlin(h, h2_w, h2_s), approximate=False)
        return _tlin(h, w3_w, w3_s)

    def _L1_attn_ref(input_data, qk, ov):
        import jax, jax.numpy as jnp
        import numpy as np
        D_MODEL = 128
        SCALE = float(np.sqrt(D_MODEL))
        S = input_data.shape[1]
        scores = jnp.einsum('bsd,de,bte->bst', input_data, qk, input_data) / SCALE
        causal = jnp.tril(jnp.ones((S, S), dtype=bool))
        scores = jnp.where(causal, scores, -jnp.inf)
        attn = jax.nn.softmax(scores, axis=-1)
        return jnp.einsum('bst,btd,de->bse', attn, input_data, ov)

    def _L1_ffn_ref(x, ln_gamma, ln_beta, mu, scale, w1, b1, w2, b2):
        import jax, jax.numpy as jnp
        import numpy as np
        LN_EPS = 1e-05
        NORM_EPS = 1e-12

        def _layernorm(x, gamma, beta):
            mu = x.mean(axis=-1, keepdims=True)
            var = ((x - mu) ** 2).mean(axis=-1, keepdims=True)
            return (x - mu) * jax.lax.rsqrt(var + LN_EPS) * gamma + beta

        def _l2norm(x, axis):
            n = jnp.sqrt((x ** 2).sum(axis=axis, keepdims=True))
            return x / jnp.maximum(n, NORM_EPS)
        B, N, D = x.shape
        _, E, S = mu.shape
        xn = _layernorm(x, ln_gamma, ln_beta)
        x_unit = _l2norm(xn, axis=-1)
        mu_unit = _l2norm(mu, axis=0)
        logits = jnp.einsum('bnd,des->bnes', x_unit * scale, mu_unit)
        dispatch = jax.nn.softmax(logits, axis=1)
        combine = jax.nn.softmax(logits.reshape(B, N, E * S), axis=-1).reshape(B, N, E, S)
        slot_in = jnp.einsum('bnd,bnes->besd', xn, dispatch)
        h = jax.nn.gelu(jnp.einsum('besd,edh->besh', slot_in, w1) + b1[None, :, None, :], approximate=False)
        slot_out = jnp.einsum('besh,ehd->besd', h, w2) + b2[None, :, None, :]
        out = jnp.einsum('besd,bnes->bnd', slot_out, combine)
        return out
    x = L0_attn_x
    x = _layernorm(x + _L0_attn_ref(x, L0_attn_q_w, L0_attn_k_w, L0_attn_v_w, L0_attn_out_w, L0_attn_out_b), axis=-1)
    x = _layernorm(x + _L0_ffn_ref(x, L0_ffn_w1_w, L0_ffn_w1_s, L0_ffn_w2_w, L0_ffn_w2_s, L0_ffn_h1_w, L0_ffn_h1_s, L0_ffn_h2_w, L0_ffn_h2_s, L0_ffn_w3_w, L0_ffn_w3_s), axis=-1)
    x = _layernorm(x + _L1_attn_ref(x, L1_attn_qk, L1_attn_ov), axis=-1)
    x = _layernorm(x + _L1_ffn_ref(x, L1_ffn_ln_gamma, L1_ffn_ln_beta, L1_ffn_mu, L1_ffn_scale, L1_ffn_w1, L1_ffn_b1, L1_ffn_w2, L1_ffn_b2), axis=-1)
    return x

_drawn_inputs = setup_inputs


def setup_inputs(seed=0):
    import zlib

    import numpy as np

    out = dict(_drawn_inputs(seed))
    spreads = {'L0_attn_out_b': (0.0, 0.1),
     'L1_ffn_ln_gamma': (1.0, 0.6),
     'L1_ffn_ln_beta': (0.0, 0.67),
     'L1_ffn_b1': (0.0, 0.8),
     'L1_ffn_b2': (0.0, 0.34)}
    factors = {'L0_ffn_w1_w': 8.0,
     'L0_ffn_w1_s': 8.0,
     'L0_ffn_w2_w': 8.0,
     'L0_ffn_w2_s': 8.0,
     'L0_ffn_h1_w': 8.0,
     'L0_ffn_h1_s': 8.0,
     'L0_ffn_h2_w': 8.0,
     'L0_ffn_h2_s': 8.0,
     'L0_ffn_w3_w': 8.0,
     'L0_ffn_w3_s': 8.0,
     'L1_ffn_mu': 8.0}
    for name, (base, spread) in spreads.items():
        noise = np.random.default_rng([zlib.crc32(name.encode()), seed]).standard_normal(out[name].shape)
        drawn = base * np.exp(spread * noise) if base else spread * noise
        out[name] = jnp.asarray(drawn.astype(out[name].dtype))
    for name, factor in factors.items():
        out[name] = (out[name] * factor).astype(out[name].dtype)
    return out
```

```python
from contextlib import ExitStack

import concourse.bass as bass
from concourse import mybir

F32 = mybir.dt.float32
BF16 = mybir.dt.bfloat16
ALU = mybir.AluOpType
ACT = mybir.ActivationFunctionType
AX_X = mybir.AxisListType.X

P = 128
B = 8
S = 1024
D = 128
NT = S // P
TT = B * NT
CH = 512
NB = 3
HID = 512
MC = HID // P

H = 16
HD = D // H
G = 4
NG = H // G
KBLK = 64
NKB = S // KBLK
ROWS = NB * NB * HD
AROWS = 96
BROWS = AROWS + NB
UNITS = 2 * NG
SCALE0 = float(HD) ** -0.5
LN_EPS = 1e-5


def wait(eng, sem, value):
    if not (isinstance(value, int) and value <= 0):
        eng.wait_ge(sem, value)


def make_identity(nc, ctx, ident, ident_done):
    block = ctx.enter_context(nc.Block())

    @block.gpsimd
    def _(pool):
        pool.memset(ident[:, :], 0.0).then_inc(ident_done, 1)
        pool.wait_ge(ident_done, 1)
        pool.affine_select(out=ident[:, :], in_=ident[:, :], compare_op=ALU.not_equal, fill=1.0, base=0,
                           pattern=[[-1, P]], channel_multiplier=1).then_inc(ident_done, 1)


def project_qkv(nc, xT, wqT, wkT, wvT, q_scr, k_scr, v_scr, stacks_zero, stacks_one):
    with ExitStack() as ctx:
        def sb(name, shape, dt):
            return ctx.enter_context(nc.sbuf_tensor(name, shape, dt))

        def sem(name):
            return ctx.enter_context(nc.semaphore(name))

        def two(name):
            return [sem(f"{name}{c}") for c in range(2)]

        w = [sb(f"w_{n}", [P, D], F32) for n in "qkv"]
        xt = sb("xt", [P, 2, CH], F32)
        parts = sb("parts", [P, 2, 2, NB, CH], BF16)
        rest = sb("rest", [P, 2, 2, CH], F32)
        v_sb = sb("v_sb", [P, 2, CH // P, D], F32)
        proj = [[ctx.enter_context(nc.psum_tensor(f"proj_{o}{c}", [P, CH], F32)) for o in "qkv"] for c in range(2)]
        zero_tile, one_tile = sb("zero_tile", [P, S], BF16), sb("one_tile", [P, S], BF16)
        tiles_set, zeroed, oned = sem("tiles_set"), sem("zeroed"), sem("oned")
        w_loaded = sem("w_loaded")
        x_loaded, projected = two("x_loaded"), two("projected")
        part1, rested, part2, part3 = two("part1"), two("rested"), two("part2"), two("part3")
        v_copied, qk_written, v_written = two("v_copied"), two("qk_written"), two("v_written")
        QK_DMAS = NB + NB + 2
        block = ctx.enter_context(nc.Block())

        def each_batch(eng, body):
            body(0)
            with eng.Fori(1, B) as b:
                body(b)

        @block.sync
        def _(sp):
            for t, src in zip(w, (wqT, wkT, wvT)):
                sp.dma_start(t[:, :], src).then_inc(w_loaded, 16)
            for c in range(2):
                sp.dma_start(xt[:, c, :], xT[:, c * CH:(c + 1) * CH]).then_inc(x_loaded[c], 16)

            def store(b, c):
                cols = slice(c * CH, (c + 1) * CH)
                for o, scr in enumerate((q_scr, k_scr)):
                    sp.wait_ge(part3[c], b * 2 + (o + 1))
                    for i in range(NB if o == 0 else NB + 2):
                        sp.dma_start(scr[b, :, i * HD:(i + 1) * HD, cols],
                                     parts[:, c, o, i % NB, :]).then_inc(qk_written[c], 16)
                sp.wait_ge(v_copied[c], b + 1)
                sp.dma_start(v_scr[b, :, c * 4:c * 4 + 4, :], v_sb[:, c, :, :]).then_inc(v_written[c], 16)

            with sp.Fori(0, B) as b:
                for c in range(2):
                    store(b, c)
            for c in range(2):
                sp.wait_ge(qk_written[c], B * QK_DMAS * 16)
                sp.wait_ge(v_written[c], B * 16)

        @block.gpsimd
        def _(pool):
            def batch(b):
                for c in range(2):
                    for o in range(2):
                        pool.wait_ge(part2[c], b * 2 + (o + 1))
                        pool.tensor_tensor(parts[:, c, o, 2, :], rest[:, c, o, :], parts[:, c, o, 1, :],
                                           ALU.subtract).then_inc(part3[c], 1)

            each_batch(pool, batch)

        @block.vector
        def _(dve):
            dve.memset(zero_tile[:, :], 0.0).then_inc(tiles_set, 1)
            dve.memset(one_tile[:, :], 1.0).then_inc(tiles_set, 1)

            def batch(b):
                for c in range(2):
                    for o in range(2):
                        wait(dve, part3[c], b * 2)
                        dve.wait_ge(part1[c], b * 2 + (o + 1))
                        dve.tensor_tensor(rest[:, c, o, :], proj[c][o][:, :], parts[:, c, o, 0, :],
                                          ALU.subtract).then_inc(rested[c], 1)

            each_batch(dve, batch)

        @block.scalar
        def _(act):
            act.wait_ge(tiles_set, 2)
            for st in stacks_zero:
                act.dma_start(st[P // 2:P, :, :], zero_tile[P // 2:P, :].unsqueeze(1).to_broadcast([P // 2, G, S])
                              ).then_inc(zeroed, 16)
            act.wait_ge(zeroed, 16 * len(stacks_zero))
            for st in stacks_one:
                act.dma_start(st[AROWS:BROWS, :, :], one_tile[AROWS:BROWS, :].unsqueeze(1).to_broadcast([NB, G, S])
                              ).then_inc(oned, 16)

            def batch(b, last):
                for c in range(2):
                    wait(act, qk_written[c], b * (QK_DMAS * 16))
                    for o in range(2):
                        act.wait_ge(projected[c], b * 3 + (o + 1))
                        act.activation(parts[:, c, o, 0, :], proj[c][o][:, :], ACT.Copy).then_inc(part1[c], 1)
                    wait(act, v_written[c], b * 16)
                    act.wait_ge(projected[c], b * 3 + 3)
                    act.activation(v_sb[:, c, :, :].rearrange("p a b -> p (a b)"), proj[c][2][:, :],
                                   ACT.Copy).then_inc(v_copied[c], 1)
                    if not last:
                        act.dma_start(xt[:, c, :], xT[:, bass.ds(b * S + (S + c * CH), CH)]).then_inc(x_loaded[c], 16)
                for c in range(2):
                    for o in range(2):
                        act.wait_ge(rested[c], b * 2 + (o + 1))
                        act.activation(parts[:, c, o, 1, :], rest[:, c, o, :], ACT.Copy).then_inc(part2[c], 1)

            batch(0, False)
            with act.Fori(1, B - 1) as b:
                batch(b, False)
            batch(B - 1, True)
            act.wait_ge(oned, 16 * len(stacks_one))

        @block.tensor
        def _(pe):
            pe.wait_ge(w_loaded, 3 * 16)

            def batch(b):
                for c in range(2):
                    pe.wait_ge(x_loaded[c], b * 16 + 16)
                    for o in range(2):
                        wait(pe, rested[c], b * 2)
                        pe.matmul(proj[c][o][:, :], w[o][:, :], xt[:, c, :], start=True,
                                  stop=True).then_inc(projected[c], 1)
                    wait(pe, v_copied[c], b)
                    for j in range(CH // P):
                        mm = pe.matmul(proj[c][2][:, j * D:(j + 1) * D], xt[:, c, j * P:(j + 1) * P], w[2][:, :],
                                       start=True, stop=True)
                    mm.then_inc(projected[c], 1)

            each_batch(pe, batch)


def head_attention(nc, ident, q_scr, k_scr, v_scr, nm_scr, q_st, k_st, o_raw, m_first, m_all, loads):
    with ExitStack() as ctx:
        def sb(name, shape, dt):
            return ctx.enter_context(nc.sbuf_tensor(name, shape, dt))

        def sem(name):
            return ctx.enter_context(nc.semaphore(name))

        QT = CH // P
        v_in = sb("v_in", [P, NT, D], F32)
        v_pad = [sb(f"v_pad{i}", [P, NT, G, 32], F32) for i in range(2)]
        prob = sb("prob", [P, 2, G, CH], F32)
        blk_max = sb("blk_max", [P, 2, G * QT, NKB], F32)
        first_max = sb("first_max", [P, G * QT], F32)
        row_max = sb("row_max", [P, G * QT], F32)
        neg_max = sb("neg_max", [P, G * QT], F32)
        neg_rest = sb("neg_rest", [P, G * QT], F32)
        neg_parts = sb("neg_parts", [P, P // (G * QT), G * QT], BF16)
        negT = sb("negT", [NB * G * QT, P], BF16)
        zeros = sb("zeros", [P, NT, G, HD], F32)
        minus = sb("minus", [P, G * QT], F32)
        oT = sb("oT", [P, CH], F32)
        ident16 = sb("ident16", [P, P], BF16)

        psum = [ctx.enter_context(nc.psum_tensor(f"bank{i}", [P, CH], F32)) for i in range(4)]
        max_ps = [ctx.enter_context(nc.psum_tensor(f"max_ps{i}", [P, 2 * CH], F32)) for i in range(2)]
        ring, acc = psum[0:3], psum[3]
        ring16 = [r[:, :].bitcast(BF16) for r in ring]

        TURNS = []
        for t in range(NT):
            TURNS += [("s", t * G + h) for h in range(G)]
            TURNS += {2: [("o", 0)], 4: [("n", 0)], 5: [None], 7: [None]}.get(t, [])
        assert len(TURNS) % len(ring) == 0

        def bank_of(turn):
            return TURNS.index(turn) % len(ring)

        def wait_bank(pe, turn, unit, no_neg):
            k = TURNS.index(turn) - len(ring)
            while TURNS[k] is None or (TURNS[k][0] == "n" and k >= 0 and no_neg):
                k -= len(ring)
            kind, n = TURNS[k]
            at = unit if k >= 0 else unit - 1
            if kind == "s":
                wait(pe, exp_done, at * (NT * G) + (n + 1))
            elif kind == "o":
                wait(pe, o_kept, at)
            else:
                wait(pe, neg_copied, at + 2)

        stack_loaded = [sem(f"stack_loaded{g}") for g in range(NG)]
        pads_set, id16_done = sem("pads_set"), sem("id16_done")
        v_loaded, v_padded = sem("v_loaded"), sem("v_padded")
        max_scored, max_taken = sem("max_scored"), sem("max_taken")
        max_done, neg_done = sem("max_done"), sem("neg_done")
        chain = sem("neg_chain")
        neg_turned, neg_copied, neg_written, bias_loaded = sem("neg_turned"), sem("neg_copied"), sem("neg_written"), sem("bias_loaded")
        scored, exp_done, pv_done = sem("scored"), sem("exp_done"), sem("pv_done")
        acc_copied, o_turned, o_kept = sem("acc_copied"), sem("o_turned"), sem("o_kept")
        block = ctx.enter_context(nc.Block())

        def each_batch(eng, body):
            body(0, True, False)
            with eng.Fori(1, B - 1) as b:
                body(b, False, False)
            body(B - 1, False, True)

        @block.sync
        def _(sp):
            def load_stacks(b, g):
                heads = slice(g * G, (g + 1) * G)
                for r in range(NB):
                    rows = slice(r * NB * HD, (r + 1) * NB * HD)
                    sp.dma_start(q_st[g][rows, :, :],
                                 q_scr[b, heads, :, :].rearrange("h r t -> r h t")).then_inc(stack_loaded[g], 16)
                    sp.dma_start(k_st[g][rows, :, :],
                                 k_scr[b, heads, r * HD:(r + NB) * HD, :].rearrange("h r t -> r h t")
                                 ).then_inc(stack_loaded[g], 16)

            def load_bias(unit, u):
                g, half = u % UNITS // 2, u % 2
                sp.wait_ge(neg_copied, unit + 1)
                sp.dma_start(nm_scr[half, :, :], negT[:, :]).then_inc(neg_written, 16)
                sp.wait_ge(neg_written, unit * 16 + 16)
                sp.dma_start(q_st[g][AROWS:BROWS, :, half * CH:(half + 1) * CH],
                             nm_scr[half, :, :].rearrange("(i h q) p -> i h (q p)", i=NB, h=G)
                             ).then_inc(bias_loaded, 16)

            load_stacks(0, 0)
            sp.dma_start(v_in[:, :, :], v_scr[0, :, :, :]).then_inc(v_loaded, 16)
            load_stacks(0, 1)
            load_bias(0, 0)

            def batch(b, first, last):
                for u in range(UNITS):
                    g = u // 2
                    if u % 2 == 0 and not (last and g >= 2):
                        wait(sp, pv_done, b * (UNITS * NT) + (u - 2) * NT)
                        load_stacks(b + (g + 2) // NG, (g + 2) % NG)
                    if u == 6 and not last:
                        wait(sp, v_padded, b * NG + NG)
                        sp.dma_start(v_in[:, :, :], v_scr[b + 1, :, :, :]).then_inc(v_loaded, 16)
                    if not (last and u == UNITS - 1):
                        load_bias(b * UNITS + (u + 1), u + 1)

            each_batch(sp, batch)

        @block.gpsimd
        def _(pool):
            pool.tensor_copy(ident16[:, :], ident[:, :]).then_inc(id16_done, 1)
            for t in (v_pad[0], v_pad[1], zeros):
                pool.memset(t[:, :, :, :], 0.0).then_inc(chain, 1)
            pool.memset(neg_parts[:, :, :], 0.0).then_inc(chain, 1)
            pool.memset(minus[:, :], -1.0).then_inc(chain, 1)
            C0 = 5
            pool.wait_ge(chain, C0)
            for i in range(2):
                pool.memset(v_pad[i][P - KBLK:P, NT - 1, :, HD:HD + 1], 1.0).then_inc(pads_set, 1)
            pool.wait_ge(pads_set, 2)

            def pad_values(b, g, group):
                wait(pool, v_loaded, b * 16 + 16)
                wait(pool, pv_done, (group - 1) * (2 * NT))
                pool.tensor_tensor(v_pad[g % 2][:, :, :, 0:HD],
                                   v_in[:, :, g * G * HD:(g + 1) * G * HD].rearrange("p t (h d) -> p t h d", d=HD),
                                   zeros[:, :, :, :], ALU.add).then_inc(v_padded, 1)

            STEPS = 6

            def negate_max(unit, tile0, u):
                u = u % UNITS
                g = u // 2
                count = unit * STEPS
                wait(pool, chain, count + C0)
                pool.wait_ge(max_done, unit * 2 + 2)
                zero = zeros[:, 0, :, 0:QT]
                flat = zeros[:, 0, 0:2, :].rearrange("p a b -> p (a b)")
                kept = [m[:, bass.ds(tile0, QT), g * G:(g + 1) * G].rearrange("p q h -> p h q") for m in (m_first, m_all)]
                pool.tensor_tensor(kept[0], first_max[:, :].rearrange("p (h q) -> p h q", h=G), zero, ALU.add).then_inc(chain, 1)
                pool.tensor_tensor(kept[1], row_max[:, :].rearrange("p (h q) -> p h q", h=G), zero, ALU.add).then_inc(chain, 1)
                pool.tensor_tensor(neg_max[:, :], row_max[:, :], minus[:, :], ALU.mult).then_inc(chain, 1)
                pool.wait_ge(chain, count + (C0 + 3))
                pool.wait_ge(neg_turned, unit)
                pool.tensor_tensor(neg_parts[:, 0, :], neg_max[:, :], flat, ALU.add).then_inc(chain, 1)
                pool.wait_ge(chain, count + (C0 + 4))
                pool.tensor_tensor(neg_rest[:, :], neg_max[:, :], neg_parts[:, 0, :], ALU.subtract).then_inc(chain, 1)
                pool.wait_ge(chain, count + (C0 + 5))
                pool.tensor_tensor(neg_parts[:, 1, :], neg_rest[:, :], flat, ALU.add).then_inc(chain, 1)
                pool.wait_ge(chain, count + (C0 + 6))
                pool.tensor_tensor(neg_parts[:, 2, :], neg_rest[:, :], neg_parts[:, 1, :],
                                   ALU.subtract).then_inc(neg_done, 1)

            pad_values(0, 0, 0)
            negate_max(0, 0, 0)

            def batch(b, first, last):
                for u in range(UNITS):
                    n = u + 1
                    if u % 2 == 0 and not (last and u == UNITS - 2):
                        g = u // 2 + 1
                        pad_values(b + g // NG, g % NG, b * NG + g)
                    if not (last and n == UNITS):
                        tile0 = b * NT + (n % 2) * QT + (NT if n == UNITS else 0)
                        negate_max(b * UNITS + n, tile0, n)

            each_batch(pool, batch)

        @block.vector
        def _(dve):
            def max_tile(unit, u, s):
                dve.wait_ge(max_scored, unit * (G * QT) + (s + 1))
                dve.tensor_reduce(blk_max[:, u % 2, s, :],
                                  max_ps[s % 2][:, :].rearrange("p (n k) -> p n k", k=KBLK),
                                  AX_X, ALU.max).then_inc(max_taken, 1)

            def row_maxima(unit, u):
                wait(dve, neg_done, unit)
                dve.wait_ge(max_taken, unit * (G * QT) + G * QT)
                dve.tensor_reduce(first_max[:, :], blk_max[:, u % 2, :, 0:NKB - 1], AX_X,
                                  ALU.max).then_inc(max_done, 1)
                dve.tensor_reduce(row_max[:, :], blk_max[:, u % 2, :, :], AX_X, ALU.max).then_inc(max_done, 1)

            def copy_acc(unit):
                dve.wait_ge(pv_done, unit * NT + NT)
                wait(dve, o_turned, unit)
                dve.tensor_copy(oT[:, :], acc[:, :]).then_inc(acc_copied, 1)

            for u in range(2):
                for s in range(G * QT):
                    max_tile(u, u, s)
                if u == 0:
                    row_maxima(0, 0)

            def batch(b, first, last):
                for u in range(UNITS):
                    unit = b * UNITS + u
                    if not (last and u == UNITS - 1):
                        row_maxima(unit + 1, u + 1)
                    for s in range(G * QT):
                        if not (last and u >= UNITS - 2):
                            if s == 0:
                                wait(dve, neg_done, unit + 1)
                            max_tile(unit + 2, u, s)
                        if s == 1 and not (first and u == 0):
                            copy_acc(unit - 1)

            each_batch(dve, batch)
            copy_acc(B * UNITS - 1)

        @block.scalar
        def _(act):
            def keep_output(unit, tile0, u):
                g = u % UNITS // 2
                act.wait_ge(o_turned, unit + 1)
                act.activation(o_raw[:, bass.ds(tile0, QT), g * G:(g + 1) * G, :],
                               ring[bank_of(("o", 0))][:, :].rearrange("p (q h c) -> p q h c", q=QT, h=G)[:, :, :, 0:HD + 1],
                               ACT.Copy).then_inc(o_kept, 1)

            def copy_neg(unit):
                act.wait_ge(neg_turned, unit + 1)
                wait(act, neg_written, unit * 16)
                act.activation(negT[:, :], ring16[bank_of(("n", 0))][0:NB * G * QT, 0:P], ACT.Copy).then_inc(neg_copied, 1)

            for dst, src, done in loads:
                act.dma_start(dst, src).then_inc(done, 16)
            copy_neg(0)

            def batch(b, first, last):
                for u in range(UNITS):
                    unit = b * UNITS + u
                    for t in range(NT):
                        tiles = b * (UNITS * NT) + (u * NT + t)
                        wait(act, pv_done, tiles - 1)
                        for h in range(G):
                            act.wait_ge(scored, b * (UNITS * NT * G) + ((u * NT + t) * G + h + 1))
                            act.activation(prob[:, t % 2, h, :], ring[bank_of(("s", t * G + h))][:, :], ACT.Exp,
                                           scale=SCALE0).then_inc(exp_done, 1)
                        if t == 2 and not (first and u == 0):
                            keep_output(unit - 1, b * NT + ((u - 1) % 2 * QT - (NT if u == 0 else 0)), u - 1)
                        if t == 4 and not (last and u == UNITS - 1):
                            copy_neg(unit + 1)

            each_batch(act, batch)
            keep_output(B * UNITS - 1, (B - 1) * NT + QT, UNITS - 1)

        @block.tensor
        def _(pe):
            def max_pair(b, unit, u, s):
                g, half, h, qt = u % UNITS // 2, u % 2, s // QT, s % QT
                if s == 0 and half == 0:
                    pe.wait_ge(stack_loaded[g], b * (2 * NB * 16) + 2 * NB * 16)
                wait(pe, max_taken, unit * (G * QT) + (s - 1))
                q0 = half * CH + qt * P
                for k in range(2):
                    mm = pe.matmul(max_ps[s % 2][:, k * CH:(k + 1) * CH], q_st[g][0:AROWS, h, q0:q0 + P],
                                   k_st[g][0:AROWS, h, k * CH:(k + 1) * CH], start=True, stop=True)
                mm.then_inc(max_scored, 1)

            def score_tile(b, u, t, h, last):
                g, half = u // 2, u % 2
                turn = ("s", t * G + h)
                wait_bank(pe, turn, b * UNITS + u, last and u == UNITS - 1)
                pe.matmul(ring[bank_of(turn)][:, :], k_st[g][0:BROWS, h, t * P:(t + 1) * P],
                          q_st[g][0:BROWS, h, half * CH:(half + 1) * CH], start=True, stop=True).then_inc(scored, 1)

            def values(b, unit, u, t):
                g = u % UNITS // 2
                if t == 0:
                    wait(pe, acc_copied, unit)
                    if u % 2 == 0:
                        pe.wait_ge(v_padded, b * NG + (g + 1))
                pe.wait_ge(exp_done, b * (UNITS * NT * G) + ((u * NT + t) * G + G))
                for h in range(G):
                    mm = pe.matmul(acc[32 * h:32 * h + 32, :], v_pad[g % 2][:, t, h, :], prob[:, t % 2, h, :],
                                   start=(t == 0), stop=(t == NT - 1))
                mm.then_inc(pv_done, 1)

            def turn_output(unit):
                pe.wait_ge(acc_copied, unit + 1)
                bank = ring[bank_of(("o", 0))]
                for q in range(QT):
                    mm = pe.transpose(bank[:, q * P:(q + 1) * P], oT[:, q * P:(q + 1) * P], ident[:, :])
                mm.then_inc(o_turned, 1)

            def turn_neg(unit):
                pe.wait_ge(neg_done, unit + 1)
                pe.transpose(ring16[bank_of(("n", 0))][:, 0:P], neg_parts[:, :, :].rearrange("p i n -> p (i n)"),
                             ident16[:, :]).then_inc(neg_turned, 1)

            pe.wait_ge(id16_done, 1)
            for u in range(2):
                for s in range(G * QT):
                    max_pair(0, u, u, s)
                if u == 0:
                    turn_neg(0)

            def batch(b, first, last):
                for u in range(UNITS):
                    unit = b * UNITS + u
                    ahead = not (last and u >= UNITS - 2)
                    for t in range(NT):
                        if t == 0:
                            pe.wait_ge(bias_loaded, unit * 16 + 16)
                        for h in range(G):
                            if h == G - 1:
                                if t > 0:
                                    values(b, unit, u, t - 1)
                                elif not (first and u == 0):
                                    values(b, unit - 1, u - 1, NT - 1)
                            score_tile(b, u, t, h, last)
                            if ahead and h < 2:
                                max_pair(b + (u + 2) // UNITS, unit + 2, u + 2, 2 * t + h)
                        if t == 2 and not (first and u == 0):
                            wait_bank(pe, ("o", 0), unit, False)
                            turn_output(unit - 1)
                        if t == 4 and not (last and u == UNITS - 1):
                            wait_bank(pe, ("n", 0), unit, False)
                            turn_neg(unit + 1)

            each_batch(pe, batch)
            values(B - 1, B * UNITS - 1, UNITS - 1, NT - 1)
            pe.wait_ge(exp_done, B * UNITS * NT * G)
            turn_output(B * UNITS - 1)


def head_denominators(nc, o_raw, m_first, m_all, recip, weights_loaded, n_loads):
    with ExitStack() as ctx:
        corr = ctx.enter_context(nc.sbuf_tensor("corr", [P, TT * H], F32))
        stage, corr_done = (ctx.enter_context(nc.semaphore(n)) for n in ("den_stage", "corr_done"))
        block = ctx.enter_context(nc.Block())
        flat = "p t h -> p (t h)"

        @block.scalar
        def _(act):
            act.wait_ge(weights_loaded, 16 * n_loads)
            act.wait_ge(stage, 1)
            act.activation(corr[:, :], corr[:, :], ACT.Exp, scale=SCALE0).then_inc(corr_done, 1)

        @block.vector
        def _(dve):
            dve.tensor_tensor(corr[:, :], m_first[:, :, :].rearrange(flat), m_all[:, :, :].rearrange(flat),
                              ALU.subtract).then_inc(stage, 1)
            dve.wait_ge(corr_done, 1)
            dve.scalar_tensor_tensor(recip[:, :], corr[:, :], 1.0, o_raw[:, :, :, HD].rearrange(flat),
                                     ALU.add, ALU.mult).then_inc(stage, 1)
            dve.wait_ge(stage, 2)
            dve.reciprocal(recip[:, :], recip[:, :]).then_inc(stage, 1)


QT = CH // P


def norm_apply(dve, src, stats, moments, rstd, dst, sems, count):
    dve.wait_ge(sems["rstd"], count + 1)
    for j in range(QT):
        op = dve.tensor_scalar(dst(j), src[:, j, :], moments[:, j, 0:1], rstd[:, j:j + 1], ALU.subtract, ALU.mult)
    return op


def norm_stats(dve, src, stats, moments, sems, count):
    for j in range(QT):
        dve.bn_stats(stats[:, j, :], src[:, j, :]).then_inc(sems["stats"], 1)
    dve.wait_ge(sems["stats"], count * QT + QT)
    dve.memset(moments[:, QT, 0:1], 0.0)
    for j in range(QT):
        dve.bn_aggr(moments[:, j, :], stats[:, j, :]).then_inc(sems["moments"], 1)


def norm_rstd(pool, moments, var_eps, rstd, eps, half, sems, count):
    pool.wait_ge(sems["moments"], count * QT + QT)
    wait(pool, sems["used"], count)
    pool.tensor_tensor(var_eps[:, :], moments[:, 0:QT, 1], eps[:, :], ALU.add).then_inc(sems["var"], 1)
    pool.wait_ge(sems["var"], count + 1)
    pool.tensor_tensor(rstd[:, :], var_eps[:, :], half[:, :], ALU.pow).then_inc(sems["rstd"], 1)


def gated_mlp(nc, ident, t, W, o_raw, recip, X):
    with ExitStack() as ctx:
        def sb(name, shape, dt=F32):
            return ctx.enter_context(nc.sbuf_tensor(name, shape, dt))

        def sem(name):
            return ctx.enter_context(nc.semaphore(name))

        wo, w1, w2, h1, h2, w3, s3, bias = (W[n] for n in ("wo", "w1", "w2", "h1", "h2", "w3", "s3", "bias"))
        scales = {n: W[n] for n in ("s1", "s2", "g1", "g2")}
        x_in = [sb(f"x_in{i}", [P, QT, D]) for i in range(2)]
        xb, oc, pre = sb("xb", [P, QT, D]), sb("oc", [P, QT, D]), sb("pre", [P, QT, D])
        x1 = [sb(f"x1_{i}", [P, QT, D]) for i in range(2)]
        oT, x1T = sb("oT_c", [P, CH]), sb("x1T", [P, CH])
        silu = sb("silu", [P, 2, CH])
        gated, hid1, hid2 = (sb(n, [P, MC, CH]) for n in ("gated", "hid1", "hid2"))
        post = sb("post", [P, QT, D])
        const = {n: sb(f"c_{n}", [P, QT]) for n in ("eps", "half")}
        ln = {k: dict(stats=sb(f"stats_{k}", [P, QT, 6]), moments=sb(f"moments_{k}", [P, QT + 1, 2]),
                      var=sb(f"var_{k}", [P, QT]), rstd=sb(f"rstd_{k}", [P, QT]),
                      sems={n: sem(f"{k}_{n}") for n in ("stats", "moments", "var", "rstd", "used")})
              for k in ("front", "back")}
        ring = [ctx.enter_context(nc.psum_tensor(f"ring{i}", [P, CH], F32)) for i in range(4)]
        turn, proj, down = (ctx.enter_context(nc.psum_tensor(n, [P, CH], F32)) for n in ("turn_c", "proj_c", "down_c"))

        const_set = sem("const_set")
        x_loaded = [sem(f"x_in_loaded{i}") for i in range(2)]
        xb_done, oc_done, o_turned, oT_done, projected = (sem(n) for n in ("xb_done", "oc_done", "o_turned2", "oT_done", "projected2"))
        pre_done, x1_done, x1_turned, x1T_done = (sem(n) for n in ("pre_done", "x1_done", "x1_turned", "x1T_done"))
        ab_done, silu_done, gated_done, hid_done, gelu_done = (sem(n) for n in ("ab_done", "silu_done", "gated_done", "hid_done", "gelu_done"))
        down_done, scaled, post_done, x2_done = (sem(n) for n in ("down_done", "scaled", "post_done", "x2_done"))
        block = ctx.enter_context(nc.Block())
        N = B * 2

        def each_pair(eng, body):
            body(0, True, False)
            with eng.Fori(1, B - 1) as b:
                body(b, False, False)
            body(B - 1, False, True)

        @block.sync
        def _(sp):
            def load_x(c, par):
                wait(sp, xb_done, c - 1)
                sp.dma_start(x_in[par][:, :, :],
                             t["x"].rearrange("b (t p) d -> p (b t) d", p=P)[:, bass.ds(c * QT, QT), :]
                             ).then_inc(x_loaded[par], 16)

            load_x(0, 0)
            load_x(1, 1)

            def pair(b, first, last):
                if not last:
                    for i in range(2):
                        load_x(b * 2 + (2 + i), i)

            each_pair(sp, pair)

        @block.gpsimd
        def _(pool):
            pool.memset(const["eps"][:, :], LN_EPS).then_inc(const_set, 1)
            pool.memset(const["half"][:, :], -0.5).then_inc(const_set, 1)
            pool.wait_ge(const_set, 2)

            def rstd(k, c):
                s = ln[k]
                norm_rstd(pool, s["moments"], s["var"], s["rstd"], const["eps"], const["half"], s["sems"], c)

            def front(c, par, b):
                pool.wait_ge(x_loaded[par], b * 16 + 16)
                wait(pool, pre_done, c)
                pool.tensor_tensor(xb[:, :, :], x_in[par][:, :, :],
                                   bias[:, :].unsqueeze(1).to_broadcast([P, QT, D]), ALU.add).then_inc(xb_done, 1)
                rstd("front", c)

            front(0, 0, 0)

            def pair(b, first, last):
                for i in range(2):
                    if not (last and i == 1):
                        front(b * 2 + (i + 1), (i + 1) % 2, b + (i + 1) // 2)
                    rstd("back", b * 2 + i)

            each_pair(pool, pair)

        @block.vector
        def _(dve):
            def divide(c):
                wait(dve, o_turned, c)
                dve.tensor_tensor(oc[:, :, :].rearrange("p t (h d) -> p (t h) d", d=HD),
                                  o_raw[:, bass.ds(c * QT, QT), :, 0:HD].rearrange("p t h d -> p (t h) d"),
                                  recip[:, bass.ds(c * (QT * H), QT * H)].unsqueeze(2).to_broadcast([P, QT * H, HD]),
                                  ALU.mult).then_inc(oc_done, 1)

            def front(c, par):
                dve.wait_ge(projected, c + 1)
                dve.wait_ge(xb_done, c + 1)
                wait(dve, x1_done, c)
                dve.tensor_tensor(pre[:, :, :], proj[:, :].rearrange("p (t d) -> p t d", d=D), xb[:, :, :],
                                  ALU.add).then_inc(pre_done, 1)
                dve.wait_ge(pre_done, c + 1)
                s = ln["front"]
                norm_stats(dve, pre, s["stats"], s["moments"], s["sems"], c)
                wait(dve, post_done, c - 1)
                op = norm_apply(dve, pre, s["stats"], s["moments"], s["rstd"], lambda j: x1[par][:, j, :], s["sems"], c)
                op.then_inc(x1_done, 1)
                dve.wait_ge(x1_done, c + 1)
                dve.sem_inc(s["sems"]["used"], 1)

            def gate(c):
                for m in range(MC):
                    dve.wait_ge(silu_done, c * MC + (m + 1))
                    dve.wait_ge(ab_done, c * (2 * MC) + (2 * m + 2))
                    if m == 0:
                        wait(dve, hid_done, c * (2 * MC) - MC)
                    dve.scalar_tensor_tensor(gated[:, m, :], ring[(2 * m + 1) % 4][:, :], scales["s2"][:, m:m + 1],
                                             silu[:, m % 2, :], ALU.mult, ALU.mult).then_inc(gated_done, 1)

            def back(c, par):
                dve.wait_ge(down_done, c + 1)
                wait(dve, x2_done, c)
                dve.tensor_tensor(post[:, :, :], down[:, :].rearrange("p (t d) -> p t d", d=D),
                                  s3[:, :].unsqueeze(1).to_broadcast([P, QT, D]), ALU.mult).then_inc(scaled, 1)
                dve.wait_ge(scaled, c + 1)
                dve.tensor_tensor(post[:, :, :], post[:, :, :], x1[par][:, :, :], ALU.add).then_inc(post_done, 1)
                dve.wait_ge(post_done, c + 1)
                s = ln["back"]
                norm_stats(dve, post, s["stats"], s["moments"], s["sems"], c)
                op = norm_apply(dve, post, s["stats"], s["moments"], s["rstd"],
                                lambda j: X[:, bass.ds(c * QT + j, 1), :].rearrange("p a d -> p (a d)"), s["sems"], c)
                op.then_inc(x2_done, 1)
                dve.wait_ge(x2_done, c + 1)
                dve.sem_inc(s["sems"]["used"], 1)

            divide(0)
            front(0, 0)
            divide(1)

            def pair(b, first, last):
                for i in range(2):
                    c = b * 2 + i
                    gate(c)
                    if not (last and i == 1):
                        front(c + 1, (i + 1) % 2)
                    if not last:
                        divide(c + 2)
                    back(c, i)

            each_pair(dve, pair)

        @block.scalar
        def _(act):
            def copy_oT(c):
                act.wait_ge(o_turned, c + 1)
                wait(act, projected, c)
                act.activation(oT[:, :], turn[:, :], ACT.Copy).then_inc(oT_done, 1)

            def copy_x1T(c):
                act.wait_ge(x1_turned, c + 1)
                wait(act, ab_done, c * (2 * MC))
                act.activation(x1T[:, :], turn[:, :], ACT.Copy).then_inc(x1T_done, 1)

            def gelu(c, n, dst, scale, m):
                act.wait_ge(hid_done, c * (2 * MC) + (n + 1))
                act.activation(dst[:, m, :], ring[n % 4][:, :], ACT.Gelu, scale=scale[:, m:m + 1]).then_inc(gelu_done, 1)

            copy_oT(0)
            copy_x1T(0)

            def pair(b, first, last):
                for i in range(2):
                    c = b * 2 + i
                    for m in range(MC):
                        act.wait_ge(ab_done, c * (2 * MC) + (2 * m + 1))
                        wait(act, gated_done, c * MC + (m - 1))
                        act.activation(silu[:, m % 2, :], ring[2 * m % 4][:, :], ACT.Silu,
                                       scale=scales["s1"][:, m:m + 1]).then_inc(silu_done, 1)
                    if not (last and i == 1):
                        copy_oT(c + 1)
                    for m in range(MC):
                        if m == 0:
                            wait(act, hid_done, c * (2 * MC))
                        gelu(c, m, hid1, scales["g1"], m)
                    for m in range(MC):
                        if m == 0:
                            wait(act, down_done, c)
                        if m == 2 and not (last and i == 1):
                            copy_x1T(c + 1)
                        gelu(c, MC + m, hid2, scales["g2"], m)

            each_pair(act, pair)

        @block.tensor
        def _(pe):
            def turn_o(c):
                pe.wait_ge(oc_done, c + 1)
                wait(pe, x1T_done, c)
                for j in range(QT):
                    mm = pe.transpose(turn[:, j * P:(j + 1) * P], oc[:, j, :], ident[:, :])
                mm.then_inc(o_turned, 1)

            def project(c):
                pe.wait_ge(oT_done, c + 1)
                wait(pe, pre_done, c)
                for j in range(QT):
                    mm = pe.matmul(proj[:, j * D:(j + 1) * D], oT[:, j * P:(j + 1) * P], wo[:, :], start=True, stop=True)
                mm.then_inc(projected, 1)

            def turn_x1(c, par):
                pe.wait_ge(x1_done, c + 1)
                pe.wait_ge(oT_done, c + 1)
                for j in range(QT):
                    mm = pe.transpose(turn[:, j * P:(j + 1) * P], x1[par][:, j, :], ident[:, :])
                mm.then_inc(x1_turned, 1)

            def gates(c):
                pe.wait_ge(x1T_done, c + 1)
                for m in range(MC):
                    for o, w in enumerate((w1, w2)):
                        if m < 2:
                            wait(pe, gelu_done, c * (2 * MC) + (2 * m + o - MC + 1))
                        elif o == 0:
                            pe.wait_ge(silu_done, c * MC + (m - 1))
                        else:
                            pe.wait_ge(gated_done, c * MC + (m - 1))
                        pe.matmul(ring[(2 * m + o) % 4][:, :], w[:, m * P:(m + 1) * P], x1T[:, :], start=True,
                                  stop=True).then_inc(ab_done, 1)

            def hidden(c, n, w, src, m):
                if n < 4:
                    pe.wait_ge(gated_done, c * MC + (3 if n < 2 else 4))
                else:
                    pe.wait_ge(gelu_done, c * (2 * MC) + (n - 3))
                for k in range(MC):
                    if n == 0:
                        pe.wait_ge(gated_done, c * MC + (k + 1))
                    if n == MC:
                        pe.wait_ge(gelu_done, c * (2 * MC) + (k + 1))
                    mm = pe.matmul(ring[n % 4][:, :], w[:, k, m * P:(m + 1) * P], src[:, k, :], start=(k == 0),
                                   stop=(k == MC - 1))
                mm.then_inc(hid_done, 1)

            def downward(c):
                wait(pe, scaled, c)
                pe.wait_ge(gelu_done, c * (2 * MC) + 2 * MC)
                for j in range(QT):
                    for k in range(MC):
                        mm = pe.matmul(down[:, j * D:(j + 1) * D], hid2[:, k, j * P:(j + 1) * P], w3[:, k, :],
                                       start=(k == 0), stop=(k == MC - 1))
                mm.then_inc(down_done, 1)

            turn_o(0)
            project(0)
            turn_x1(0, 0)

            def pair(b, first, last):
                for i in range(2):
                    c = b * 2 + i
                    ahead = not (last and i == 1)
                    gates(c)
                    if ahead:
                        turn_o(c + 1)
                    for m in range(MC):
                        if m == 2 and ahead:
                            project(c + 1)
                        hidden(c, m, h1, gated, m)
                    for m in range(MC):
                        if m == 2 and ahead:
                            turn_x1(c + 1, (i + 1) % 2)
                        hidden(c, MC + m, h2, hid1, m)
                    downward(c)

            each_pair(pe, pair)


def causal_attention(nc, ident, W, X):
    with ExitStack() as ctx:
        def sb(name, shape, dt=F32):
            return ctx.enter_context(nc.sbuf_tensor(name, shape, dt))

        def sem(name):
            return ctx.enter_context(nc.semaphore(name))

        def ps(name, cols=CH):
            return ctx.enter_context(nc.psum_tensor(name, [P, cols], F32))

        SC = float(D) ** -0.5
        PIECES = 6
        TURNS = sum((i // QT) + 1 for i in range(NT))
        qk, ov, mask = W["qk"], W["ov"], sb("mask", [P, P])
        xs = [sb(f"xs{i}", [P, NT, D]) for i in range(2)]
        xT = [sb(f"xT{i}", [P, S]) for i in range(2)]
        yT = [sb(f"yT{i}", [P, S]) for i in range(2)]
        xov = [sb(f"xov{i}", [P, NT, D]) for i in range(2)]
        prob = [sb(f"prob_d{i}", [P, S]) for i in range(2)]
        pT = [sb(f"pT{i}", [P, NT, P]) for i in range(2)]
        top, neg, total, inv = (sb(n, [P, 2]) for n in ("row_top", "row_neg", "row_total", "row_inv"))
        pre = sb("pre_d", [P, QT, D])
        eps, half = sb("eps_d", [P, QT]), sb("half_d", [P, QT])
        stats, moments, var, rstd = sb("stats_d", [P, QT, 6]), sb("moments_d", [P, QT + 1, 2]), sb("var_d", [P, QT]), sb("rstd_d", [P, QT])
        sems = {n: sem(f"d_{n}") for n in ("stats", "moments", "var", "rstd", "used")}
        score = [ps(f"score{i}", 2 * CH) for i in range(2)]
        turned, piece, outp = [ps(f"turned{i}") for i in range(2)], ps("piece"), ps("outp")
        const_set, mask_set = sem("const_set_d"), sem("mask_set")
        xs_done, made, copied = sem("xs_done"), sem("piece_made"), sem("piece_copied")
        scored, masked, topped, negged, exp_done = (sem(n) for n in ("scored_d", "masked", "topped", "negged", "exp_done_d"))
        turn_done, turn_copied, pv_done, inv_done, pre_done, x_done = (sem(n) for n in ("turn_done", "turn_copied", "pv_done_d", "inv_done", "pre_done_d", "x_done"))
        block = ctx.enter_context(nc.Block())

        def turns_to(i):
            return sum((k // QT) + 1 for k in range(i + 1)) if i >= 0 else -sum((NT + k) // QT + 1 for k in range(i + 1, 0))

        def each_pair(eng, body):
            body(0, True, False)
            with eng.Fori(1, B // 2 - 1) as b:
                body(b, False, False)
            body(B // 2 - 1, False, True)

        @block.gpsimd
        def _(pool):
            pool.memset(mask[:, :], 0.0).then_inc(const_set, 1)
            pool.memset(eps[:, :], LN_EPS).then_inc(const_set, 1)
            pool.memset(half[:, :], -0.5).then_inc(const_set, 1)
            pool.wait_ge(const_set, 3)
            pool.affine_select(out=mask[:, :], in_=mask[:, :], compare_op=ALU.is_ge, fill=-1e30, base=0,
                               pattern=[[-1, P]], channel_multiplier=1).then_inc(mask_set, 1)

            def pair(b, first, last):
                for i in range(4):
                    norm_rstd(pool, moments, var, rstd, eps, half, sems, b * 4 + i)

            each_pair(pool, pair)

        @block.scalar
        def _(act):
            def take_x(bb, par):
                wait(act, pre_done, bb * NT - NT)
                act.activation(xs[par][:, :, :], X[:, bass.ds(bb * NT, NT), :], ACT.Copy).then_inc(xs_done, 1)

            def exps(bb, i):
                n = bb * NT + i
                act.wait_ge(negged, n + 1)
                wait(act, turn_done, bb * TURNS + turns_to(i - 2))
                wait(act, pre_done, n - 1)
                act.activation(prob[i % 2][:, 0:(i + 1) * P], score[i % 2][:, 0:(i + 1) * P], ACT.Exp, scale=SC,
                               bias=neg[:, i % 2:i % 2 + 1], accum_out=total[:, i % 2:i % 2 + 1]).then_inc(exp_done, 1)

            take_x(0, 0)
            exps(0, 0)

            def batch(bb, par, first, last):
                for i in range(NT):
                    if i == 1 and not last:
                        take_x(bb + 1, 1 - par)
                    for p in range(i // QT + 1):
                        k = turns_to(i - 1) + p
                        act.wait_ge(turn_done, bb * TURNS + (k + 1))
                        if p == 0:
                            wait(act, pv_done, bb * NT + (i - 1))
                        n = min(QT, i + 1 - p * QT)
                        act.activation(pT[i % 2][:, p * QT:p * QT + n, :].rearrange("p a b -> p (a b)"),
                                       turned[k % 2][:, 0:n * P], ACT.Copy).then_inc(turn_copied, 1)
                    if not (last and i == NT - 1):
                        exps(bb + (i + 1) // NT, (i + 1) % NT)

            def pair(b, first, last):
                for i in range(2):
                    batch(b * 2 + i, i, first and i == 0, last and i == 1)

            each_pair(act, pair)

        @block.vector
        def _(dve):
            def softmax_top(bb, i):
                n = bb * NT + i
                dve.wait_ge(scored, n + 1)
                diag = score[i % 2][:, i * P:(i + 1) * P]
                dve.tensor_tensor(diag, diag, mask[:, :], ALU.add).then_inc(masked, 1)
                dve.wait_ge(masked, n + 1)
                dve.tensor_reduce(top[:, i % 2:i % 2 + 1], score[i % 2][:, 0:(i + 1) * P], AX_X, ALU.max).then_inc(topped, 1)
                dve.wait_ge(topped, n + 1)
                wait(dve, exp_done, n - 1)
                dve.tensor_scalar(neg[:, i % 2:i % 2 + 1], top[:, i % 2:i % 2 + 1], -SC, None, ALU.mult).then_inc(negged, 1)

            def copy_piece(bb, f, par):
                dve.wait_ge(made, bb * PIECES + (f + 1))
                if f == 0:
                    wait(dve, scored, bb * NT - NT)
                if f == 4:
                    wait(dve, pv_done, bb * NT - NT)
                h = f % 2
                dst = (xT[par][:, h * CH:(h + 1) * CH], yT[par][:, h * CH:(h + 1) * CH],
                       xov[par][:, h * QT:(h + 1) * QT, :].rearrange("p a b -> p (a b)"))[f // 2]
                dve.tensor_copy(dst, piece[:, :]).then_inc(copied, 1)

            def residual(bb, i, par):
                n = bb * NT + i
                dve.wait_ge(exp_done, n + 1)
                dve.reciprocal(inv[:, i % 2:i % 2 + 1], total[:, i % 2:i % 2 + 1]).then_inc(inv_done, 1)
                dve.wait_ge(inv_done, n + 1)
                dve.wait_ge(pv_done, n + 1)
                if i % QT == 0:
                    wait(dve, x_done, bb * 2 + i // QT)
                dve.scalar_tensor_tensor(pre[:, i % QT, :], outp[:, 0:D], inv[:, i % 2:i % 2 + 1], xs[par][:, i, :],
                                         ALU.mult, ALU.add).then_inc(pre_done, 1)
                if i % QT == QT - 1:
                    g = bb * 2 + i // QT
                    dve.wait_ge(pre_done, n + 1)
                    norm_stats(dve, pre, stats, moments, sems, g)
                    op = norm_apply(dve, pre, stats, moments, rstd,
                                    lambda j: X[:, bass.ds(g * QT + j, 1), :].rearrange("p a d -> p (a d)"), sems, g)
                    op.then_inc(x_done, 1)
                    dve.wait_ge(x_done, g + 1)
                    dve.sem_inc(sems["used"], 1)

            for f in range(PIECES):
                copy_piece(0, f, 0)
            dve.wait_ge(mask_set, 1)
            softmax_top(0, 0)

            def batch(bb, par, first, last):
                for i in range(NT):
                    if not (last and i == NT - 1):
                        softmax_top(bb + (i + 1) // NT, (i + 1) % NT)
                    if i >= 1:
                        residual(bb, i - 1, par)
                    elif not first:
                        residual(bb - 1, NT - 1, 1 - par)
                    if i >= 2 and not last:
                        copy_piece(bb + 1, i - 2, 1 - par)

            def pair(b, first, last):
                for i in range(2):
                    batch(b * 2 + i, i, first and i == 0, last and i == 1)

            each_pair(dve, pair)
            residual(B - 1, NT - 1, 1)

        @block.tensor
        def _(pe):
            def make_piece(bb, f, par):
                if f == 0:
                    pe.wait_ge(xs_done, bb + 1)
                wait(pe, copied, bb * PIECES + f)
                h = f % 2
                if f // 2 == 1:
                    mm = pe.matmul(piece[:, :], qk[:, :], xT[par][:, h * CH:(h + 1) * CH], start=True, stop=True)
                else:
                    for j in range(QT):
                        dst = piece[:, j * P:(j + 1) * P]
                        if f // 2 == 0:
                            mm = pe.transpose(dst, xs[par][:, h * QT + j, :], ident[:, :])
                        else:
                            mm = pe.matmul(dst, xT[par][:, (h * QT + j) * P:(h * QT + j + 1) * P], ov[:, :],
                                           start=True, stop=True)
                mm.then_inc(made, 1)

            def scores(bb, i, par):
                if i == 0:
                    pe.wait_ge(copied, bb * PIECES + 4)
                wait(pe, exp_done, bb * NT + (i - 1))
                for k in range(i // QT + 1):
                    w = min(CH, (i + 1) * P - k * CH)
                    mm = pe.matmul(score[i % 2][:, k * CH:k * CH + w], yT[par][:, i * P:(i + 1) * P],
                                   xT[par][:, k * CH:k * CH + w], start=True, stop=True)
                mm.then_inc(scored, 1)

            def turn_probs(bb, i):
                pe.wait_ge(exp_done, bb * NT + (i + 1))
                for p in range(i // QT + 1):
                    k = turns_to(i - 1) + p
                    wait(pe, turn_copied, bb * TURNS + (k - 1))
                    for j in range(min(QT, i + 1 - p * QT)):
                        mm = pe.transpose(turned[k % 2][:, j * P:(j + 1) * P],
                                          prob[i % 2][:, (p * QT + j) * P:(p * QT + j + 1) * P], ident[:, :])
                    mm.then_inc(turn_done, 1)

            def values(bb, i, par):
                pe.wait_ge(turn_copied, bb * TURNS + turns_to(i))
                wait(pe, pre_done, bb * NT + i)
                if i == 0:
                    pe.wait_ge(copied, bb * PIECES + PIECES)
                for j in range(i + 1):
                    mm = pe.matmul(outp[:, 0:D], pT[i % 2][:, j, :], xov[par][:, j, :], start=(j == 0), stop=(j == i))
                mm.then_inc(pv_done, 1)

            for f in range(PIECES):
                make_piece(0, f, 0)
            scores(0, 0, 0)

            def batch(bb, par, first, last):
                for i in range(NT):
                    if i < NT - 1:
                        scores(bb, i + 1, par)
                    elif not last:
                        scores(bb + 1, 0, 1 - par)
                    if i >= 1:
                        values(bb, i - 1, par)
                    elif not first:
                        values(bb - 1, NT - 1, 1 - par)
                    if i >= 2 and not last:
                        make_piece(bb + 1, i - 2, 1 - par)
                    turn_probs(bb, i)

            def pair(b, first, last):
                for i in range(2):
                    batch(b * 2 + i, i, first and i == 0, last and i == 1)

            each_pair(pe, pair)
            values(B - 1, NT - 1, 1)


def soft_experts(nc, ident, W, X, out):
    with ExitStack() as ctx:
        def sb(name, shape, dt=F32):
            return ctx.enter_context(nc.sbuf_tensor(name, shape, dt))

        def sem(name):
            return ctx.enter_context(nc.semaphore(name))

        def ps(name, cols=CH):
            return ctx.enter_context(nc.psum_tensor(name, [P, cols], F32))

        NE, NS, EH = 16, 16, 32
        SL = NE * NS
        EG = P // EH
        GR = NE // EG
        GS = EG * NS
        TINY = 1e-24

        mu, gamma, beta, scale, ew1, ew2, b1, b2 = (W[n] for n in ("mu", "gamma", "beta", "mscale", "ew1", "ew2", "eb1", "eb2"))
        mu_sq, mu_inv, mu_unit = (sb(n, [P, SL]) for n in ("mu_sq", "mu_inv", "mu_unit"))
        ones = sb("ones_e", [P, P])
        own = sb("own", [P, GR, GS])
        eps, half = sb("eps_e", [P, NT]), sb("half_e", [P, SL])
        xm, xg, sq, xu = (sb(n, [P, NT, D]) for n in ("xm", "xg", "sq", "xu"))
        xn = [sb(f"xn{i}", [P, NT, D]) for i in range(2)]
        f_stats, f_moments, f_var, f_rstd = sb("f_stats", [P, NT, 6]), sb("f_moments", [P, NT + 1, 2]), sb("f_var", [P, NT]), sb("f_rstd", [P, NT])
        sumsq, guarded, inv_norm = (sb(n, [P, NT]) for n in ("sumsq", "guarded", "inv_norm"))
        xuT, comb = sb("xuT", [P, S]), sb("comb", [P, NT, SL])
        row_top, row_neg = sb("row_top_e", [P, NT]), sb("row_neg_e", [P, NT])
        row_sum, row_inv = [sb(f"row_sum{i}", [P, NT]) for i in range(2)], [sb(f"row_inv{i}", [P, NT]) for i in range(2)]
        combT = [sb(f"combT{i}", [P, 2, S]) for i in range(2)]
        dispT, disp = sb("dispT", [P, 2, S]), sb("disp", [P, NT, SL])
        col_top, col_neg, col_sum, col_inv = (sb(n, [P, 2]) for n in ("col_top", "col_neg", "col_sum", "col_inv"))
        slotT, act_h, own_h, slot_out = sb("slotT", [P, SL]), sb("act_h", [P, GR, GS]), sb("own_h", [P, GR, GS]), sb("slot_out", [P, 2, D])
        pre = sb("pre_e", [P, QT, D])
        fin = [sb(f"fin{i}", [P, NT, D]) for i in range(2)]
        l_stats, l_moments, l_var, l_rstd = sb("l_stats", [P, QT, 6]), sb("l_moments", [P, QT + 1, 2]), sb("l_var", [P, QT]), sb("l_rstd", [P, QT])

        ring, colp = [ps(f"ring_e{i}") for i in range(2)], ps("colp", 2 * CH)
        slot_ps, hid_ps, so_ps, out_ps = ps("slot_ps"), ps("hid_ps"), ps("so_ps"), ps("out_ps")
        fs = {n: sem(f"f_{n}") for n in ("stats", "moments", "var", "rstd", "used")}
        ls = {n: sem(f"l_{n}") for n in ("stats", "moments", "var", "rstd", "used")}
        const_set, mu_step, own_set = sem("const_set_e"), sem("mu_step"), sem("own_set")
        xm_done, xg_done, xn_done, sq_done, sumsq_done, guard_done, inorm_done, xu_done = (sem(n) for n in (
            "xm_done", "xg_done", "xn_done", "sq_done", "sumsq_done", "guard_done", "inorm_done", "xu_done"))
        ring_ready, ring_free = [sem(f"ring_ready{i}") for i in range(2)], [sem(f"ring_free{i}") for i in range(2)]
        row_topped, row_negged, row_exp, row_inved = sem("row_topped"), sem("row_negged"), sem("row_exp"), sem("row_inved")
        col_scored, col_topped, col_negged, col_exp, col_inved, disp_normed = (sem(n) for n in (
            "col_scored", "col_topped", "col_negged", "col_exp", "col_inved", "disp_normed"))
        slotted, slot_copied, hidden_done, gelu_done, owned, so_done, so_added = (sem(n) for n in (
            "slotted", "slot_copied", "hidden_done", "gelu_done_e", "owned", "so_done", "so_added"))
        combined, added, fin_done, stored = sem("combined"), sem("added"), sem("fin_done"), [sem(f"stored{i}") for i in range(2)]
        block = ctx.enter_context(nc.Block())

        FRONT = ["xT0", "xT1", "rl0", "rl1", "rl2", "rl3", "cT0", "cT1", "cT2", "cT3"]
        BOTH = ["xT0", "xT1", "dT0", "dT1", "rl0", "rl1", "dT2", "dT3", "rl2", "rl3", "cT0", "cT1", "cT2", "cT3"]
        BACK = ["dT0", "dT1", "dT2", "dT3"]

        def task(name, b):
            tasks, before = (FRONT, 0) if b is None else (BACK if isinstance(b, int) and b == B - 1 else BOTH, None)
            k = tasks.index(name)
            if before is None:
                before = b * (len(BOTH) // 2) + len(FRONT) // 2
            return k % 2, before + k // 2

        def each_pair(eng, body):
            body(0, True, False)
            with eng.Fori(1, B // 2 - 1) as b:
                body(b, False, False)
            body(B // 2 - 1, False, True)

        def steps(eng, step):
            def pair(b, first, last):
                for i in range(2):
                    step(b * 2 + i, i, last and i == 1, last)
            each_pair(eng, pair)

        @block.sync
        def _(sp):
            def step(b, par, last, last_pair):
                sp.wait_ge(fin_done, b * 2 + 2)
                sp.dma_start(out.rearrange("b (t p) d -> p (b t) d", p=P)[:, bass.ds(b * NT, NT), :],
                             fin[par][:, :, :]).then_inc(stored[par], 16)

            steps(sp, step)
            for i in range(2):
                sp.wait_ge(stored[i], B // 2 * 16)

        @block.gpsimd
        def _(pool):
            pool.memset(eps[:, :], LN_EPS).then_inc(const_set, 1)
            pool.memset(half[:, :], -0.5).then_inc(const_set, 1)
            pool.memset(ones[:, :], 1.0).then_inc(const_set, 1)
            pool.wait_ge(const_set, 3)
            pool.tensor_tensor(mu_sq[:, :], mu[:, :], mu[:, :], ALU.mult).then_inc(mu_step, 1)
            pool.wait_ge(mu_step, 3)
            pool.tensor_tensor(mu_inv[:, :], mu_sq[:, :], half[:, :], ALU.pow).then_inc(mu_step, 1)

            def wide(v):
                return v[:, :].unsqueeze(1).to_broadcast([P, NT, D])

            def norm(b, par):
                pool.wait_ge(fs["moments"], b * NT + NT)
                pool.tensor_tensor(f_var[:, :], f_moments[:, 0:NT, 1], eps[:, :], ALU.add).then_inc(fs["var"], 1)
                pool.wait_ge(fs["var"], b + 1)
                wait(pool, xm_done, b)
                pool.tensor_tensor(f_rstd[:, :], f_var[:, :], half[:, 0:NT], ALU.pow).then_inc(fs["rstd"], 1)
                pool.wait_ge(xm_done, b + 1)
                pool.tensor_tensor(xg[:, :, :], xm[:, :, :], wide(gamma), ALU.mult).then_inc(xg_done, 1)
                pool.wait_ge(xg_done, b + 1)
                wait(pool, slotted, b - 1)
                pool.tensor_tensor(xn[par][:, :, :], xg[:, :, :], wide(beta), ALU.add).then_inc(xn_done, 1)
                pool.wait_ge(xn_done, b + 1)
                wait(pool, sumsq_done, b)
                pool.tensor_tensor(sq[:, :, :], xn[par][:, :, :], xn[par][:, :, :], ALU.mult).then_inc(sq_done, 1)
                pool.wait_ge(guard_done, b + 1)
                wait(pool, xu_done, b)
                pool.tensor_tensor(inv_norm[:, :], guarded[:, :], half[:, 0:NT], ALU.pow).then_inc(inorm_done, 1)

            norm(0, 0)
            norm(1, 1)

            def step(b, par, last, last_pair):
                if not last_pair:
                    norm(b + 2, par)
                for g in range(2):
                    norm_rstd(pool, l_moments, l_var, l_rstd, eps[:, 0:QT], half[:, 0:QT], ls, b * 2 + g)

            steps(pool, step)

        @block.vector
        def _(dve):
            dve.memset(own[:, :, :], 0.0).then_inc(own_set, 1)
            dve.wait_ge(own_set, 1)
            for e in range(EG):
                dve.memset(own[e * EH:(e + 1) * EH, :, e * NS:(e + 1) * NS], 1.0).then_inc(own_set, 1)
            dve.wait_ge(mu_step, 2)
            dve.tensor_scalar(mu_sq[:, :], slot_ps[:, 0:SL], TINY, None, ALU.max).then_inc(mu_step, 1)
            dve.wait_ge(mu_step, 4)
            dve.scalar_tensor_tensor(mu_unit[:, :], mu[:, :], scale[:, 0:1], mu_inv[:, :], ALU.mult, ALU.mult).then_inc(mu_step, 1)

            def norm(b, par):
                for j in range(NT):
                    dve.bn_stats(f_stats[:, j, :], X[:, bass.ds(b * NT + j, 1), :].rearrange("p a d -> p (a d)")).then_inc(fs["stats"], 1)
                dve.wait_ge(fs["stats"], b * NT + NT)
                dve.memset(f_moments[:, NT, 0:1], 0.0)
                for j in range(NT):
                    dve.bn_aggr(f_moments[:, j, :], f_stats[:, j, :]).then_inc(fs["moments"], 1)
                dve.wait_ge(fs["rstd"], b + 1)
                wait(dve, xg_done, b)
                for j in range(NT):
                    op = dve.tensor_scalar(xm[:, j, :], X[:, bass.ds(b * NT + j, 1), :].rearrange("p a d -> p (a d)"),
                                           f_moments[:, j, 0:1], f_rstd[:, j:j + 1], ALU.subtract, ALU.mult)
                op.then_inc(xm_done, 1)
                dve.wait_ge(sq_done, b + 1)
                dve.tensor_reduce(sumsq[:, :], sq[:, :, :], AX_X, ALU.add).then_inc(sumsq_done, 1)
                dve.wait_ge(sumsq_done, b + 1)
                wait(dve, inorm_done, b)
                dve.tensor_scalar(guarded[:, :], sumsq[:, :], TINY, None, ALU.max).then_inc(guard_done, 1)
                dve.wait_ge(inorm_done, b + 1)

            def unit(b, par, before):
                wait(dve, ring_ready[1], before)
                dve.tensor_tensor(xu[:, :, :], xn[par][:, :, :], inv_norm[:, :].unsqueeze(2).to_broadcast([P, NT, D]),
                                  ALU.mult).then_inc(xu_done, 1)

            def ring_wait(eng, name, s):
                i, before = task(name, s)
                eng.wait_ge(ring_ready[i], before + 1)
                return i

            def copy_x(s):
                for q in range(2):
                    i = ring_wait(dve, f"xT{q}", s)
                    if q == 0 and s is not None:
                        dve.wait_ge(col_scored, s * 2 + 2)
                    dve.tensor_copy(xuT[:, q * CH:(q + 1) * CH], ring[i][:, :]).then_inc(ring_free[i], 1)

            def row_max(b, s, q):
                i = ring_wait(dve, f"rl{q}", s)
                wait(dve, row_negged, b * 4 + q)
                dve.tensor_reduce(row_top[:, 2 * q:2 * q + 2], ring[i][:, :].rearrange("p (t s) -> p t s", s=SL), AX_X,
                                  ALU.max).then_inc(row_topped, 1)
                dve.wait_ge(row_topped, b * 4 + (q + 1))
                if q == 0:
                    wait(dve, row_exp, b * NT)
                dve.tensor_scalar(row_neg[:, 2 * q:2 * q + 2], row_top[:, 2 * q:2 * q + 2], -1.0, None,
                                  ALU.mult).then_inc(row_negged, 1)

            def col_max(b, h):
                dve.wait_ge(col_scored, b * 2 + (h + 1))
                dve.tensor_reduce(col_top[:, h:h + 1], colp[:, :], AX_X, ALU.max).then_inc(col_topped, 1)
                dve.wait_ge(col_topped, b * 2 + (h + 1))
                dve.tensor_scalar(col_neg[:, h:h + 1], col_top[:, h:h + 1], -1.0, None, ALU.mult).then_inc(col_negged, 1)

            def col_norm(b, h):
                dve.wait_ge(col_exp, b * 2 + (h + 1))
                dve.reciprocal(col_inv[:, h:h + 1], col_sum[:, h:h + 1]).then_inc(col_inved, 1)
                dve.wait_ge(col_inved, b * 2 + (h + 1))
                dve.tensor_scalar(dispT[:, h, :], dispT[:, h, :], col_inv[:, h:h + 1], None, ALU.mult).then_inc(disp_normed, 1)

            def rows_inv(b, par):
                dve.wait_ge(row_exp, b * NT + NT)
                dve.reciprocal(row_inv[par][:, :], row_sum[par][:, :]).then_inc(row_inved, 1)

            def finish(b, par, g):
                n = b * 2 + g
                dve.wait_ge(combined, n + 1)
                dve.wait_ge(row_inved, b + 1)
                wait(dve, fin_done, n)
                for j in range(QT):
                    tile = g * QT + j
                    op = dve.scalar_tensor_tensor(pre[:, j, :], out_ps[:, j * D:(j + 1) * D], row_inv[par][:, tile:tile + 1],
                                                  X[:, bass.ds(b * NT + tile, 1), :].rearrange("p a d -> p (a d)"),
                                                  ALU.mult, ALU.add)
                op.then_inc(added, 1)
                dve.wait_ge(added, n + 1)
                norm_stats(dve, pre, l_stats, l_moments, ls, n)
                if g == 0:
                    wait(dve, stored[par], b * 8 - par * 8)
                op = norm_apply(dve, pre, l_stats, l_moments, l_rstd, lambda j: fin[par][:, g * QT + j, :], ls, n)
                op.then_inc(fin_done, 1)
                dve.wait_ge(fin_done, n + 1)
                dve.sem_inc(ls["used"], 1)

            norm(0, 0)
            unit(0, 0, 0)
            copy_x(None)
            for q in range(4):
                row_max(0, None, q)
            norm(1, 1)
            unit(1, 1, 1)
            for h in range(2):
                col_max(0, h)
                col_norm(0, h)

            def step(b, par, last, last_pair):
                nxt = 1 - par
                rows_inv(b, par)
                if not last:
                    copy_x(b)
                    for q in range(4):
                        row_max(b + 1, b, q)
                dve.wait_ge(slotted, b + 1)
                dve.tensor_copy(slotT[:, :], slot_ps[:, 0:SL]).then_inc(slot_copied, 1)
                if not last:
                    col_max(b + 1, 0)
                    col_norm(b + 1, 0)
                dve.wait_ge(gelu_done, b * GR + GR)
                dve.tensor_tensor(own_h[:, :, :], act_h[:, :, :], own[:, :, :], ALU.mult).then_inc(owned, 1)
                if not last:
                    col_max(b + 1, 1)
                dve.wait_ge(so_done, b + 1)
                dve.tensor_tensor(slot_out[:, :, :], so_ps[:, 0:2 * D].rearrange("p (h d) -> p h d", h=2), b2[:, :, :],
                                  ALU.add).then_inc(so_added, 1)
                if not last:
                    col_norm(b + 1, 1)
                if not last_pair:
                    norm(b + 2, par)
                    unit(b + 2, par, task("xT1", b)[1] + 1)
                for g in range(2):
                    finish(b, par, g)

            steps(dve, step)

        @block.scalar
        def _(act):
            def ring_wait(name, s):
                i, before = task(name, s)
                act.wait_ge(ring_ready[i], before + 1)
                return i

            def row_exps(b, par, s, q):
                i, _ = task(f"rl{q}", s)
                act.wait_ge(row_negged, b * 4 + (q + 1))
                if q == 0:
                    i3, before = task("cT3", None if s is None or (isinstance(s, int) and s == 0) else s - 1)
                    if s is not None:
                        act.wait_ge(ring_ready[i3], before + 1)
                    wait(act, row_inved, b - 1)
                for j in range(2):
                    tile = 2 * q + j
                    op = act.activation(comb[:, tile, :], ring[i][:, j * SL:(j + 1) * SL], ACT.Exp,
                                        bias=row_neg[:, tile:tile + 1], accum_out=row_sum[par][:, tile:tile + 1])
                    op.then_inc(row_exp, 1)
                act.wait_ge(row_exp, b * NT + (2 * q + 2))
                act.sem_inc(ring_free[i], 1)

            def col_exps(b, h, s):
                act.wait_ge(col_negged, b * 2 + (h + 1))
                act.activation(dispT[:, h, :], colp[:, :], ACT.Exp, bias=col_neg[:, h:h + 1],
                               accum_out=col_sum[:, h:h + 1]).then_inc(col_exp, 1)

            def turn_copies(names, dst, s):
                for q in names:
                    i = ring_wait(q, s)
                    act.activation(dst(int(q[2])), ring[i][:, :], ACT.Copy).then_inc(ring_free[i], 1)

            def comb_dst(par):
                return lambda q: combT[par][:, q // 2, (q % 2) * CH:(q % 2 + 1) * CH]

            def disp_dst(q):
                return disp[:, 2 * q:2 * q + 2, :].rearrange("p t s -> p (t s)")

            for q in range(4):
                row_exps(0, 0, None, q)
            turn_copies(["cT0", "cT1"], comb_dst(0), None)
            col_exps(0, 0, None)
            turn_copies(["cT2", "cT3"], comb_dst(0), None)
            col_exps(0, 1, None)

            def step(b, par, last, last_pair):
                nxt = 1 - par
                wait(act, slotted, b)
                turn_copies(["dT0", "dT1"], disp_dst, b)
                if not last:
                    row_exps(b + 1, nxt, b, 0)
                    row_exps(b + 1, nxt, b, 1)
                turn_copies(["dT2", "dT3"], disp_dst, b)
                if not last:
                    row_exps(b + 1, nxt, b, 2)
                    row_exps(b + 1, nxt, b, 3)
                    col_exps(b + 1, 0, b)
                    wait(act, combined, b * 2)
                    turn_copies(["cT0", "cT1"], comb_dst(nxt), b)
                act.wait_ge(hidden_done, b + 1)
                wait(act, owned, b)
                for g in range(GR):
                    act.activation(act_h[:, g, :], hid_ps[:, g * GS:(g + 1) * GS], ACT.Gelu, bias=b1[:, g:g + 1]).then_inc(gelu_done, 1)
                if not last:
                    col_exps(b + 1, 1, b)
                    turn_copies(["cT2", "cT3"], comb_dst(nxt), b)

            steps(act, step)

        @block.tensor
        def _(pe):
            def fill(name, s, ops):
                i, before = task(name, s)
                wait(pe, ring_free[i], before)
                ops(ring[i]).then_inc(ring_ready[i], 1)

            def turn(src):
                def ops(bank):
                    for j in range(QT):
                        mm = pe.transpose(bank[:, j * P:(j + 1) * P], src(j), ident[:, :])
                    return mm
                return ops

            def turn_x(b, s):
                pe.wait_ge(xu_done, b + 1)
                for q in range(2):
                    fill(f"xT{q}", s, turn(lambda j: xu[:, q * QT + j, :]))

            def row_logits(b, s, qs):
                if qs[0] == 0:
                    for q in range(2):
                        i, before = task(f"xT{q}", s)
                        pe.wait_ge(ring_free[i], before + 1)
                for q in qs:
                    def ops(bank):
                        for j in range(2):
                            tile = 2 * q + j
                            mm = pe.matmul(bank[:, j * SL:(j + 1) * SL], xuT[:, tile * P:(tile + 1) * P], mu_unit[:, :],
                                           start=True, stop=True)
                        return mm
                    fill(f"rl{q}", s, ops)

            def col_logits(b, h):
                wait(pe, col_exp, b * 2 + h)
                for k in range(2):
                    mm = pe.matmul(colp[:, k * CH:(k + 1) * CH], mu_unit[:, h * P:(h + 1) * P], xuT[:, k * CH:(k + 1) * CH],
                                   start=True, stop=True)
                mm.then_inc(col_scored, 1)

            def turn_comb(b, s, qs):
                pe.wait_ge(row_exp, b * NT + NT)
                for q in qs:
                    fill(f"cT{q}", s, turn(lambda j: comb[:, (q % 2) * QT + j, (q // 2) * P:(q // 2 + 1) * P]))

            def turn_disp(b, qs):
                pe.wait_ge(disp_normed, b * 2 + 2)
                for q in qs:
                    fill(f"dT{q}", b, turn(lambda j: dispT[:, j % 2, (2 * q + j // 2) * P:(2 * q + j // 2 + 1) * P]))

            def slots(b, par):
                for q in (2, 3):
                    i, before = task(f"dT{q}", b)
                    pe.wait_ge(ring_free[i], before + 1)
                wait(pe, slot_copied, b)
                for j in range(NT):
                    mm = pe.matmul(slot_ps[:, 0:SL], xn[par][:, j, :], disp[:, j, :], start=(j == 0), stop=(j == NT - 1))
                mm.then_inc(slotted, 1)

            def experts_in(b):
                pe.wait_ge(slot_copied, b + 1)
                wait(pe, gelu_done, b * GR)
                for g in range(GR):
                    mm = pe.matmul(hid_ps[:, g * GS:(g + 1) * GS], ew1[:, g, :], slotT[:, g * GS:(g + 1) * GS], start=True, stop=True)
                mm.then_inc(hidden_done, 1)

            def experts_out(b):
                pe.wait_ge(owned, b + 1)
                wait(pe, so_added, b)
                for g in range(GR):
                    p0 = GS * (g % 2)
                    mm = pe.matmul(so_ps[p0:p0 + GS, (g // 2) * D:(g // 2 + 1) * D], own_h[:, g, :], ew2[:, g, :], start=True, stop=True)
                mm.then_inc(so_done, 1)

            def combine(b, par, g):
                if g == 0:
                    pe.wait_ge(so_added, b + 1)
                wait(pe, added, b * 2 + g)
                for j in range(QT):
                    for h in range(2):
                        mm = pe.matmul(out_ps[:, j * D:(j + 1) * D], combT[par][:, h, (g * QT + j) * P:(g * QT + j + 1) * P],
                                       slot_out[:, h, :], start=(h == 0), stop=(h == 1))
                mm.then_inc(combined, 1)

            pe.wait_ge(const_set, 3)
            pe.wait_ge(mu_step, 1)
            pe.matmul(slot_ps[:, 0:SL], ones[:, :], mu_sq[:, :], start=True, stop=True).then_inc(mu_step, 1)
            turn_x(0, None)
            pe.wait_ge(mu_step, 5)
            row_logits(0, None, (0, 1, 2, 3))
            turn_comb(0, None, (0, 1))
            col_logits(0, 0)
            turn_comb(0, None, (2, 3))
            col_logits(0, 1)

            def step(b, par, last, last_pair):
                if not last:
                    turn_x(b + 1, b)
                turn_disp(b, (0, 1))
                if not last:
                    row_logits(b + 1, b, (0, 1))
                turn_disp(b, (2, 3))
                if not last:
                    row_logits(b + 1, b, (2, 3))
                slots(b, par)
                if not last:
                    col_logits(b + 1, 0)
                experts_in(b)
                if not last:
                    turn_comb(b + 1, b, (0, 1))
                    col_logits(b + 1, 1)
                experts_out(b)
                i, before = task("cT3", None if isinstance(b, int) and b == 0 else b - 1)
                pe.wait_ge(ring_free[i], before + 1)
                combine(b, par, 0)
                if not last:
                    turn_comb(b + 1, b, (2, 3))
                combine(b, par, 1)

            steps(pe, step)


def weight_tiles(nc, ctx, t, loaded):
    def row(name):
        return t[name].rearrange("(a d) -> a d", a=1)

    W, loads = {}, []

    def tile(name, shape, src, part=None):
        if name not in W:
            W[name] = ctx.enter_context(nc.sbuf_tensor(f"w_{name}", shape, F32))
        dst = W[name][tuple(slice(None) for _ in shape)] if part is None else W[name][:, part, :]
        loads.append((dst, src, loaded))

    tile("wo", [P, D], t["woT"])
    tile("w1", [P, HID], t["w1T"])
    tile("w2", [P, HID], t["w2T"])
    for name, src in (("h1", "h1T"), ("h2", "h2T")):
        tile(name, [P, MC, HID], t[src].rearrange("(k p) n -> p k n", p=P))
    tile("w3", [P, MC, D], t["w3T"].rearrange("(k p) n -> p k n", p=P))
    for name in ("s1", "s2", "g1", "g2"):
        tile(name, [P, MC], t[name])
    for name, src in (("bias", "out_b"), ("s3", "s3"), ("gamma", "gamma"), ("beta", "beta")):
        tile(name, [P, D], row(src).to_broadcast([P, D]))
    tile("mscale", [P, 1], row("mscale").to_broadcast([P, 1]))
    tile("qk", [P, D], t["qk"])
    tile("ov", [P, D], t["ov"])
    tile("mu", [P, 256], t["mu"].rearrange("d e s -> d (e s)"))
    for name in ("ew1", "ew2"):
        tile(name, [P, 4, P], t[name])
    tile("eb1", [P, 4], t["eb1"])
    for half in range(2):
        tile("eb2", [P, 2, D], t["eb2"][half * 8:half * 8 + 8, :].unsqueeze(1).to_broadcast([8, 16, D]), half)
    return W, loads


def build(nc, t, out):
    def dram(name, shape, dt):
        return nc.dram_tensor(name, shape, dt, kind="Internal").ap()

    q_scr = dram("q_scr", (B, H, NB * HD, S), BF16)
    k_scr = dram("k_scr", (B, H, (NB + 2) * HD, S), BF16)
    v_scr = dram("v_scr", (B, P, NT, D), F32)
    nm_scr = dram("nm_scr", (2, NB * G * QT, P), BF16)
    with ExitStack() as top:
        def sb(ctx, name, shape, dt=F32):
            return ctx.enter_context(nc.sbuf_tensor(name, shape, dt))

        ident = sb(top, "ident", [P, P])
        ident_done, weights_loaded = (top.enter_context(nc.semaphore(n)) for n in ("ident_done", "weights_loaded"))
        with ExitStack() as ctx:
            make_identity(nc, ctx, ident, ident_done)
        X = sb(top, "X", [P, TT, D])
        W, loads = weight_tiles(nc, top, t, weights_loaded)
        with ExitStack() as ctx:
            o_raw = sb(ctx, "o_raw", [P, TT, H, HD + 1])
            recip = sb(ctx, "recip", [P, TT * H])
            with ExitStack() as inner:
                in_x = X[:, :, :].rearrange("p t d -> p (t d)").bitcast(BF16).rearrange("p (g h s) -> p g h s", g=NG, h=G)
                q_st = [in_x[:, g, :, :] for g in range(NG)]
                k_st = [sb(inner, f"k_stack{g}", [P, G, S], BF16) for g in range(NG)]
                project_qkv(nc, t["xT"], t["wqT"], t["wkT"], t["wvT"], q_scr, k_scr, v_scr, q_st + k_st, k_st)
                m_first, m_all = sb(inner, "m_first", [P, TT, H]), sb(inner, "m_all", [P, TT, H])
                head_attention(nc, ident, q_scr, k_scr, v_scr, nm_scr, q_st, k_st, o_raw, m_first, m_all, loads)
                head_denominators(nc, o_raw, m_first, m_all, recip, weights_loaded, len(loads))
            gated_mlp(nc, ident, t, W, o_raw, recip, X)
        causal_attention(nc, ident, W, X)
        soft_experts(nc, ident, W, X, out)


def kernel(**inputs):
    import numpy as np
    import concourse.bacc as bacc
    from concourse.bass_utils import run_bass_kernel_spmd

    def laid(name):
        return np.ascontiguousarray(inputs[name])

    x = laid("L0_attn_x")
    arrays = {"x": x, "xT": np.ascontiguousarray(x.reshape(B * S, D).T)}
    for name, src in (("wqT", "L0_attn_q_w"), ("wkT", "L0_attn_k_w"), ("wvT", "L0_attn_v_w"), ("woT", "L0_attn_out_w"),
                      ("w1T", "L0_ffn_w1_w"), ("w2T", "L0_ffn_w2_w"), ("h1T", "L0_ffn_h1_w"), ("h2T", "L0_ffn_h2_w"),
                      ("w3T", "L0_ffn_w3_w")):
        arrays[name] = np.ascontiguousarray(laid(src).T)
    for name, src in (("out_b", "L0_attn_out_b"), ("s1", "L0_ffn_w1_s"), ("s2", "L0_ffn_w2_s"), ("g1", "L0_ffn_h1_s"),
                      ("g2", "L0_ffn_h2_s"), ("s3", "L0_ffn_w3_s"), ("qk", "L1_attn_qk"), ("ov", "L1_attn_ov"),
                      ("gamma", "L1_ffn_ln_gamma"), ("beta", "L1_ffn_ln_beta"), ("mu", "L1_ffn_mu"),
                      ("mscale", "L1_ffn_scale"), ("ew1", "L1_ffn_w1"), ("eb1", "L1_ffn_b1"), ("ew2", "L1_ffn_w2"),
                      ("eb2", "L1_ffn_b2")):
        arrays[name] = laid(src)
    for name in ("s1", "s2", "g1", "g2"):
        arrays[name] = np.ascontiguousarray(arrays[name].reshape(MC, P).T)
    arrays["ew1"] = np.ascontiguousarray(arrays["ew1"].reshape(4, 4, D, 32).transpose(2, 0, 1, 3).reshape(D, 4, P))
    arrays["ew2"] = np.ascontiguousarray(arrays["ew2"].reshape(4, P, D).transpose(1, 0, 2))
    arrays["eb1"] = np.ascontiguousarray(arrays["eb1"].reshape(4, P).T)
    nc = bacc.Bacc("TRN2", target_bir_lowering=False, num_devices=1)
    given, fed = {}, {}
    for name, a in arrays.items():
        fed[f"in_{name}"] = a
        given[name] = nc.dram_tensor(f"in_{name}", a.shape, mybir.dt.from_np(a.dtype), kind="ExternalInput").ap()
    out = nc.dram_tensor("out", (B, S, D), F32, kind="ExternalOutput").ap()
    build(nc, given, out)
    return run_bass_kernel_spmd(nc, [fed], core_ids=[0]).results[0]["out"]
```

```python
from contextlib import ExitStack

import concourse.bass as bass
from concourse import mybir

F32 = mybir.dt.float32
BF16 = mybir.dt.bfloat16
ALU = mybir.AluOpType
ACT = mybir.ActivationFunctionType
AX_X = mybir.AxisListType.X

P = 128
B = 8
S = 1024
D = 128
NT = S // P
TT = B * NT
CH = 512
NB = 3
HID = 512
MC = HID // P

H = 16
HD = D // H
G = 4
NG = H // G
KBLK = 64
NKB = S // KBLK
ROWS = NB * NB * HD
AROWS = 96
BROWS = AROWS + NB
QK_DMAS = NB + NB + 2
UNITS = 2 * NG
SCALE0 = float(HD) ** -0.5
LN_EPS = 1e-5


def wait(eng, sem, value):
    if not (isinstance(value, int) and value <= 0):
        eng.wait_ge(sem, value)


def make_identity(nc, ctx, ident, ident16, ident_done):
    block = ctx.enter_context(nc.Block())

    @block.gpsimd
    def _(pool):
        pool.memset(ident[:, :], 0.0).then_inc(ident_done, 1)
        pool.wait_ge(ident_done, 1)
        pool.affine_select(out=ident[:, :], in_=ident[:, :], compare_op=ALU.not_equal, fill=1.0, base=0,
                           pattern=[[-1, P]], channel_multiplier=1).then_inc(ident_done, 1)
        pool.wait_ge(ident_done, 2)
        pool.tensor_copy(ident16[:, :], ident[:, :]).then_inc(ident_done, 1)


def load_stacks(sp, b, g, q_scr, k_scr, q_st, k_st, stack_loaded):
    heads = slice(g * G, (g + 1) * G)
    for r in range(NB):
        rows = slice(r * NB * HD, (r + 1) * NB * HD)
        sp.dma_start(q_st[g][rows, :, :], q_scr[b, heads, :, :].rearrange("h r t -> r h t")).then_inc(stack_loaded[g], 16)
        sp.dma_start(k_st[g][rows, :, :],
                     k_scr[b, heads, r * HD:(r + NB) * HD, :].rearrange("h r t -> r h t")).then_inc(stack_loaded[g], 16)


def store_parts(sp, b, o, parts, scr, written):
    for i in range(NB if o == 0 else NB + 2):
        sp.dma_start(scr[b, :, i * HD:(i + 1) * HD, :], parts[:, o, i % NB, :]).then_inc(written, 16)


def project_qkv(nc, xT, wqT, wkT, wvT, q_scr, k_scr, v_scr, q_st, k_st, stack_loaded, parts, v_sb, qk_written, v_written):
    with ExitStack() as ctx:
        def sb(name, shape, dt):
            return ctx.enter_context(nc.sbuf_tensor(name, shape, dt))

        def sem(name):
            return ctx.enter_context(nc.semaphore(name))

        def two(name):
            return [sem(f"{name}{c}") for c in range(2)]

        w = [sb(f"w_{n}", [P, D], F32) for n in "qkv"]
        xt = sb("xt", [P, 2, CH], F32)
        rest = sb("rest", [P, 2, 2, CH], F32)
        proj = [[ctx.enter_context(nc.psum_tensor(f"proj_{o}{c}", [P, CH], F32)) for o in "qkv"] for c in range(2)]
        zeroed = sem("zeroed")
        w_loaded = sem("w_loaded")
        x_loaded, projected = two("x_loaded"), two("projected")
        part1, rested, part2, part3 = two("part1"), two("rested"), two("part2"), two("part3")
        v_copied = two("v_copied")
        block = ctx.enter_context(nc.Block())

        def each_batch(eng, body):
            for par in range(2):
                body(0, par)
            with eng.Fori(1, B // 2) as pair:
                for par in range(2):
                    body(pair, par)

        @block.sync
        def _(sp):
            for t, src in zip(w, (wqT, wkT, wvT)):
                sp.dma_start(t[:, :], src).then_inc(w_loaded, 16)
            for c in range(2):
                sp.dma_start(xt[:, c, :], xT[:, c * CH:(c + 1) * CH]).then_inc(x_loaded[c], 16)

            def store(pair, par):
                b = pair * 2 + par
                for o, scr in enumerate((q_scr, k_scr)):
                    for c in range(2):
                        sp.wait_ge(part3[c], b * 2 + (o + 1))
                    store_parts(sp, b, o, parts[:, par, :, :, :], scr, qk_written[par])
                for c in range(2):
                    sp.wait_ge(v_copied[c], b + 1)
                sp.dma_start(v_scr[b, :, :, :], v_sb[:, par, :, :]).then_inc(v_written[par], 16)

            for par in range(2):
                store(0, par)
            sp.wait_ge(zeroed, 2)
            sp.wait_ge(qk_written[0], QK_DMAS * 16)
            load_stacks(sp, 0, 0, q_scr, k_scr, q_st, k_st, stack_loaded)
            with sp.Fori(1, B // 2 - 1) as pair:
                for par in range(2):
                    store(pair, par)
            store(B // 2 - 1, 0)
        @block.gpsimd
        def _(pool):
            def batch(pair, par):
                b = pair * 2 + par
                for c in range(2):
                    for o in range(2):
                        pool.wait_ge(part2[c], b * 2 + (o + 1))
                        pool.tensor_tensor(parts[:, par, o, 2, c * CH:(c + 1) * CH], rest[:, c, o, :],
                                           parts[:, par, o, 1, c * CH:(c + 1) * CH],
                                           ALU.subtract).then_inc(part3[c], 1)

            each_batch(pool, batch)

        @block.vector
        def _(dve):
            def zero_rows(groups):
                for g in groups:
                    for st in (q_st[g], k_st[g]):
                        dve.memset(st[P // 2:AROWS, :, :], 0.0).then_inc(zeroed, 1)

            def batch(pair, par):
                b = pair * 2 + par
                for c in range(2):
                    for o in range(2):
                        wait(dve, part3[c], b * 2)
                        dve.wait_ge(part1[c], b * 2 + (o + 1))
                        dve.tensor_tensor(rest[:, c, o, :], proj[c][o][:, :], parts[:, par, o, 0, c * CH:(c + 1) * CH],
                                          ALU.subtract).then_inc(rested[c], 1)

            zero_rows((0, 1))
            batch(0, 0)
            zero_rows((2, 3))
            batch(0, 1)
            with dve.Fori(1, B // 2) as pair:
                for par in range(2):
                    batch(pair, par)

        @block.scalar
        def _(act):
            def batch(pair, par, last=False):
                b = pair * 2 + par
                wait(act, qk_written[par], pair * (QK_DMAS * 16))
                wait(act, v_written[par], pair * 16)
                for c in range(2):
                    cols = slice(c * CH, (c + 1) * CH)
                    for o in range(2):
                        act.wait_ge(projected[c], b * 3 + (o + 1))
                        act.activation(parts[:, par, o, 0, cols], proj[c][o][:, :], ACT.Copy).then_inc(part1[c], 1)
                    act.wait_ge(projected[c], b * 3 + 3)
                    act.activation(v_sb[:, par, c * 4:c * 4 + 4, :].rearrange("p a b -> p (a b)"), proj[c][2][:, :],
                                   ACT.Copy).then_inc(v_copied[c], 1)
                    if not (last and par == 1):
                        act.dma_start(xt[:, c, :], xT[:, bass.ds(b * S + (S + c * CH), CH)]).then_inc(x_loaded[c], 16)
                for c in range(2):
                    cols = slice(c * CH, (c + 1) * CH)
                    for o in range(2):
                        act.wait_ge(rested[c], b * 2 + (o + 1))
                        act.activation(parts[:, par, o, 1, cols], rest[:, c, o, :], ACT.Copy).then_inc(part2[c], 1)

            for par in range(2):
                batch(0, par)
            with act.Fori(1, B // 2 - 1) as pair:
                for par in range(2):
                    batch(pair, par)
            for par in range(2):
                batch(B // 2 - 1, par, True)

        @block.tensor
        def _(pe):
            pe.wait_ge(w_loaded, 3 * 16)

            def batch(pair, par):
                b = pair * 2 + par
                for c in range(2):
                    pe.wait_ge(x_loaded[c], b * 16 + 16)
                    for o in range(2):
                        wait(pe, rested[c], b * 2)
                        pe.matmul(proj[c][o][:, :], w[o][:, :], xt[:, c, :], start=True,
                                  stop=True).then_inc(projected[c], 1)
                    wait(pe, v_copied[c], b)
                    for j in range(CH // P):
                        mm = pe.matmul(proj[c][2][:, j * D:(j + 1) * D], xt[:, c, j * P:(j + 1) * P], w[2][:, :],
                                       start=True, stop=True)
                    mm.then_inc(projected[c], 1)

            each_batch(pe, batch)


def head_attention(nc, ident, ident16, q_scr, k_scr, v_scr, nm_scr, q_st, k_st, stack_loaded,
                   parts, v_sb, qk_written, v_written, o_raw, m_first, m_all, loads):
    with ExitStack() as ctx:
        def sb(name, shape, dt):
            return ctx.enter_context(nc.sbuf_tensor(name, shape, dt))

        def sem(name):
            return ctx.enter_context(nc.semaphore(name))

        QT = CH // P
        v_in = sb("v_in", [P, NT, D], F32)
        v_pad = [sb(f"v_pad{i}", [P, NT, G, 32], F32) for i in range(2)]
        prob = sb("prob", [P, 2, G, CH], F32)
        blk_max = sb("blk_max", [P, 2, G * QT, NKB], F32)
        first_max = sb("first_max", [P, G * QT], F32)
        row_max = sb("row_max", [P, G * QT], F32)
        neg_max = sb("neg_max", [P, G * QT], F32)
        neg_rest = sb("neg_rest", [P, G * QT], F32)
        neg_parts = sb("neg_parts", [P, P // (G * QT), G * QT], BF16)
        negT = sb("negT", [NB * G * QT, P], BF16)
        zeros = sb("zeros", [P, NT, G, HD], F32)
        minus = sb("minus", [P, G * QT], F32)
        oT = sb("oT", [P, CH], F32)

        psum = [ctx.enter_context(nc.psum_tensor(f"bank{i}", [P, CH], F32)) for i in range(4)]
        max_ps = [ctx.enter_context(nc.psum_tensor(f"max_ps{i}", [P, 2 * CH], F32)) for i in range(2)]
        ring, acc = psum[0:3], psum[3]
        ring16 = [r[:, :].bitcast(BF16) for r in ring]

        TURNS = []
        for t in range(NT):
            TURNS += [("s", t * G + h) for h in range(G)]
            TURNS += {2: [("o", 0)], 4: [("n", 0)], 5: [None], 7: [None]}.get(t, [])
        assert len(TURNS) % len(ring) == 0

        def bank_of(turn):
            return TURNS.index(turn) % len(ring)

        def wait_bank(pe, turn, unit, no_neg):
            k = TURNS.index(turn) - len(ring)
            while TURNS[k] is None or (TURNS[k][0] == "n" and k >= 0 and no_neg):
                k -= len(ring)
            kind, n = TURNS[k]
            at = unit if k >= 0 else unit - 1
            if kind == "s":
                wait(pe, exp_done, at * (NT * G) + (n + 1))
            elif kind == "o":
                wait(pe, o_kept, at)
            else:
                wait(pe, neg_copied, at + 2)

        pads_set, ones_set = sem("pads_set"), sem("ones_set")
        v_loaded, v_padded = sem("v_loaded"), sem("v_padded")
        max_scored, max_taken = sem("max_scored"), sem("max_taken")
        max_done, neg_done = sem("max_done"), sem("neg_done")
        chain = sem("neg_chain")
        neg_turned, neg_copied, neg_written, bias_loaded = sem("neg_turned"), sem("neg_copied"), sem("neg_written"), sem("bias_loaded")
        scored, exp_done, pv_done = sem("scored"), sem("exp_done"), sem("pv_done")
        acc_copied, o_turned, o_kept = sem("acc_copied"), sem("o_turned"), sem("o_kept")
        block = ctx.enter_context(nc.Block())

        def each_batch(eng, body):
            body(0, True, False)
            with eng.Fori(1, B - 1) as b:
                body(b, False, False)
            body(B - 1, False, True)

        @block.sync
        def _(sp):
            def load_bias(unit, u):
                g, half = u % UNITS // 2, u % 2
                sp.wait_ge(neg_copied, unit + 1)
                sp.dma_start(nm_scr[half, :, :], negT[:, :]).then_inc(neg_written, 16)
                sp.wait_ge(neg_written, unit * 16 + 16)
                sp.dma_start(q_st[g][AROWS:BROWS, :, half * CH:(half + 1) * CH],
                             nm_scr[half, :, :].rearrange("(i h q) p -> i h (q p)", i=NB, h=G)
                             ).then_inc(bias_loaded, 16)

            for o, scr in enumerate((q_scr, k_scr)):
                store_parts(sp, B - 1, o, parts[:, 1, :, :, :], scr, qk_written[1])
            sp.dma_start(v_scr[B - 1, :, :, :], v_sb[:, 1, :, :]).then_inc(v_written[1], 16)
            for par in range(2):
                sp.wait_ge(qk_written[par], B // 2 * QK_DMAS * 16)
                sp.wait_ge(v_written[par], B // 2 * 16)
            sp.dma_start(v_in[:, :, :], v_scr[0, :, :, :]).then_inc(v_loaded, 16)
            load_stacks(sp, 0, 1, q_scr, k_scr, q_st, k_st, stack_loaded)
            load_bias(0, 0)

            def batch(b, first, last):
                for u in range(UNITS):
                    g = u // 2
                    if u % 2 == 0 and not (last and g >= 2):
                        wait(sp, pv_done, b * (UNITS * NT) + (u - 2) * NT)
                        load_stacks(sp, b + (g + 2) // NG, (g + 2) % NG, q_scr, k_scr, q_st, k_st, stack_loaded)
                    if u == 6 and not last:
                        wait(sp, v_padded, b * NG + NG)
                        sp.dma_start(v_in[:, :, :], v_scr[b + 1, :, :, :]).then_inc(v_loaded, 16)
                    if not (last and u == UNITS - 1):
                        load_bias(b * UNITS + (u + 1), u + 1)

            each_batch(sp, batch)

        @block.gpsimd
        def _(pool):
            for t in (v_pad[0], v_pad[1], zeros):
                pool.memset(t[:, :, :, :], 0.0).then_inc(chain, 1)
            pool.memset(neg_parts[:, :, :], 0.0).then_inc(chain, 1)
            pool.memset(minus[:, :], -1.0).then_inc(chain, 1)
            C0 = 5
            pool.wait_ge(chain, C0)
            for i in range(2):
                pool.memset(v_pad[i][P - KBLK:P, NT - 1, :, HD:HD + 1], 1.0).then_inc(pads_set, 1)
            pool.wait_ge(pads_set, 2)

            def pad_values(b, g, group):
                wait(pool, v_loaded, b * 16 + 16)
                wait(pool, pv_done, (group - 1) * (2 * NT))
                pool.tensor_tensor(v_pad[g % 2][:, :, :, 0:HD],
                                   v_in[:, :, g * G * HD:(g + 1) * G * HD].rearrange("p t (h d) -> p t h d", d=HD),
                                   zeros[:, :, :, :], ALU.add).then_inc(v_padded, 1)

            STEPS = 6

            def negate_max(unit, tile0, u):
                u = u % UNITS
                g = u // 2
                count = unit * STEPS
                wait(pool, chain, count + C0)
                pool.wait_ge(max_done, unit * 2 + 2)
                zero = zeros[:, 0, :, 0:QT]
                flat = zeros[:, 0, 0:2, :].rearrange("p a b -> p (a b)")
                kept = [m[:, bass.ds(tile0, QT), g * G:(g + 1) * G].rearrange("p q h -> p h q") for m in (m_first, m_all)]
                pool.tensor_tensor(kept[0], first_max[:, :].rearrange("p (h q) -> p h q", h=G), zero, ALU.add).then_inc(chain, 1)
                pool.tensor_tensor(kept[1], row_max[:, :].rearrange("p (h q) -> p h q", h=G), zero, ALU.add).then_inc(chain, 1)
                pool.tensor_tensor(neg_max[:, :], row_max[:, :], minus[:, :], ALU.mult).then_inc(chain, 1)
                pool.wait_ge(chain, count + (C0 + 3))
                pool.wait_ge(neg_turned, unit)
                pool.tensor_tensor(neg_parts[:, 0, :], neg_max[:, :], flat, ALU.add).then_inc(chain, 1)
                pool.wait_ge(chain, count + (C0 + 4))
                pool.tensor_tensor(neg_rest[:, :], neg_max[:, :], neg_parts[:, 0, :], ALU.subtract).then_inc(chain, 1)
                pool.wait_ge(chain, count + (C0 + 5))
                pool.tensor_tensor(neg_parts[:, 1, :], neg_rest[:, :], flat, ALU.add).then_inc(chain, 1)
                pool.wait_ge(chain, count + (C0 + 6))
                pool.tensor_tensor(neg_parts[:, 2, :], neg_rest[:, :], neg_parts[:, 1, :],
                                   ALU.subtract).then_inc(neg_done, 1)

            def ones_rows(g):
                pool.memset(k_st[g][AROWS:BROWS, :, :], 1.0).then_inc(ones_set, 1)

            ones_rows(0)
            pool.wait_ge(ones_set, 1)
            negate_max(0, 0, 0)
            pad_values(0, 0, 0)
            pool.wait_ge(v_padded, 1)
            for g in range(1, NG):
                ones_rows(g)
            pool.wait_ge(ones_set, NG)

            def batch(b, first, last):
                for u in range(UNITS):
                    n = u + 1
                    if u % 2 == 0 and not (last and u == UNITS - 2):
                        g = u // 2 + 1
                        pad_values(b + g // NG, g % NG, b * NG + g)
                    if not (last and n == UNITS):
                        tile0 = b * NT + (n % 2) * QT + (NT if n == UNITS else 0)
                        negate_max(b * UNITS + n, tile0, n)

            each_batch(pool, batch)

        @block.vector
        def _(dve):
            def max_tile(unit, u, s):
                dve.wait_ge(max_scored, unit * (G * QT) + (s + 1))
                dve.tensor_reduce(blk_max[:, u % 2, s, :],
                                  max_ps[s % 2][:, :].rearrange("p (n k) -> p n k", k=KBLK),
                                  AX_X, ALU.max).then_inc(max_taken, 1)

            def row_maxima(unit, u):
                wait(dve, neg_done, unit)
                dve.wait_ge(max_taken, unit * (G * QT) + G * QT)
                dve.tensor_reduce(first_max[:, :], blk_max[:, u % 2, :, 0:NKB - 1], AX_X,
                                  ALU.max).then_inc(max_done, 1)
                dve.tensor_reduce(row_max[:, :], blk_max[:, u % 2, :, :], AX_X, ALU.max).then_inc(max_done, 1)

            def copy_acc(unit):
                dve.wait_ge(pv_done, unit * NT + NT)
                wait(dve, o_turned, unit)
                dve.tensor_copy(oT[:, :], acc[:, :]).then_inc(acc_copied, 1)

            for u in range(2):
                for s in range(G * QT):
                    max_tile(u, u, s)
                if u == 0:
                    row_maxima(0, 0)

            def batch(b, first, last):
                for u in range(UNITS):
                    unit = b * UNITS + u
                    if not (last and u == UNITS - 1):
                        row_maxima(unit + 1, u + 1)
                    for s in range(G * QT):
                        if not (last and u >= UNITS - 2):
                            if s == 0:
                                wait(dve, neg_done, unit + 1)
                            max_tile(unit + 2, u, s)
                        if s == 1 and not (first and u == 0):
                            copy_acc(unit - 1)

            each_batch(dve, batch)
            copy_acc(B * UNITS - 1)

        @block.scalar
        def _(act):
            def keep_output(unit, tile0, u):
                g = u % UNITS // 2
                act.wait_ge(o_turned, unit + 1)
                act.activation(o_raw[:, bass.ds(tile0, QT), g * G:(g + 1) * G, :],
                               ring[bank_of(("o", 0))][:, :].rearrange("p (q h c) -> p q h c", q=QT, h=G)[:, :, :, 0:HD + 1],
                               ACT.Copy).then_inc(o_kept, 1)

            def copy_neg(unit):
                act.wait_ge(neg_turned, unit + 1)
                wait(act, neg_written, unit * 16)
                act.activation(negT[:, :], ring16[bank_of(("n", 0))][0:NB * G * QT, 0:P], ACT.Copy).then_inc(neg_copied, 1)

            for dst, src, done in loads:
                act.dma_start(dst, src).then_inc(done, 16)
            copy_neg(0)

            def batch(b, first, last):
                for u in range(UNITS):
                    unit = b * UNITS + u
                    for t in range(NT):
                        tiles = b * (UNITS * NT) + (u * NT + t)
                        wait(act, pv_done, tiles - 1)
                        for h in range(G):
                            act.wait_ge(scored, b * (UNITS * NT * G) + ((u * NT + t) * G + h + 1))
                            act.activation(prob[:, t % 2, h, :], ring[bank_of(("s", t * G + h))][:, :], ACT.Exp,
                                           scale=SCALE0).then_inc(exp_done, 1)
                        if t == 2 and not (first and u == 0):
                            keep_output(unit - 1, b * NT + ((u - 1) % 2 * QT - (NT if u == 0 else 0)), u - 1)
                        if t == 4 and not (last and u == UNITS - 1):
                            copy_neg(unit + 1)

            each_batch(act, batch)
            keep_output(B * UNITS - 1, (B - 1) * NT + QT, UNITS - 1)

        @block.tensor
        def _(pe):
            def max_pair(b, unit, u, s):
                g, half, h, qt = u % UNITS // 2, u % 2, s // QT, s % QT
                if s == 0 and half == 0:
                    pe.wait_ge(stack_loaded[g], b * (2 * NB * 16) + 2 * NB * 16)
                wait(pe, max_taken, unit * (G * QT) + (s - 1))
                q0 = half * CH + qt * P
                for k in range(2):
                    mm = pe.matmul(max_ps[s % 2][:, k * CH:(k + 1) * CH], q_st[g][0:AROWS, h, q0:q0 + P],
                                   k_st[g][0:AROWS, h, k * CH:(k + 1) * CH], start=True, stop=True)
                mm.then_inc(max_scored, 1)

            def score_tile(b, u, t, h, last):
                g, half = u // 2, u % 2
                turn = ("s", t * G + h)
                wait_bank(pe, turn, b * UNITS + u, last and u == UNITS - 1)
                pe.matmul(ring[bank_of(turn)][:, :], k_st[g][0:BROWS, h, t * P:(t + 1) * P],
                          q_st[g][0:BROWS, h, half * CH:(half + 1) * CH], start=True, stop=True).then_inc(scored, 1)

            def values(b, unit, u, t):
                g = u % UNITS // 2
                if t == 0:
                    wait(pe, acc_copied, unit)
                    if u % 2 == 0:
                        pe.wait_ge(v_padded, b * NG + (g + 1))
                pe.wait_ge(exp_done, b * (UNITS * NT * G) + ((u * NT + t) * G + G))
                for h in range(G):
                    mm = pe.matmul(acc[32 * h:32 * h + 32, :], v_pad[g % 2][:, t, h, :], prob[:, t % 2, h, :],
                                   start=(t == 0), stop=(t == NT - 1))
                mm.then_inc(pv_done, 1)

            def turn_output(unit):
                pe.wait_ge(acc_copied, unit + 1)
                bank = ring[bank_of(("o", 0))]
                for q in range(QT):
                    mm = pe.transpose(bank[:, q * P:(q + 1) * P], oT[:, q * P:(q + 1) * P], ident[:, :])
                mm.then_inc(o_turned, 1)

            def turn_neg(unit):
                pe.wait_ge(neg_done, unit + 1)
                pe.transpose(ring16[bank_of(("n", 0))][:, 0:P], neg_parts[:, :, :].rearrange("p i n -> p (i n)"),
                             ident16[:, :]).then_inc(neg_turned, 1)

            for u in range(2):
                for s in range(G * QT):
                    max_pair(0, u, u, s)
                if u == 0:
                    turn_neg(0)

            def batch(b, first, last):
                for u in range(UNITS):
                    unit = b * UNITS + u
                    ahead = not (last and u >= UNITS - 2)
                    for t in range(NT):
                        if t == 0:
                            pe.wait_ge(bias_loaded, unit * 16 + 16)
                        for h in range(G):
                            if h == G - 1:
                                if t > 0:
                                    values(b, unit, u, t - 1)
                                elif not (first and u == 0):
                                    values(b, unit - 1, u - 1, NT - 1)
                            score_tile(b, u, t, h, last)
                            if ahead and h < 2:
                                max_pair(b + (u + 2) // UNITS, unit + 2, u + 2, 2 * t + h)
                        if t == 2 and not (first and u == 0):
                            wait_bank(pe, ("o", 0), unit, False)
                            turn_output(unit - 1)
                        if t == 4 and not (last and u == UNITS - 1):
                            wait_bank(pe, ("n", 0), unit, False)
                            turn_neg(unit + 1)

            each_batch(pe, batch)
            values(B - 1, B * UNITS - 1, UNITS - 1, NT - 1)
            pe.wait_ge(exp_done, B * UNITS * NT * G)
            turn_output(B * UNITS - 1)


def head_denominators(nc, o_raw, m_first, m_all, denom, weights_loaded, n_loads):
    with ExitStack() as ctx:
        corr = ctx.enter_context(nc.sbuf_tensor("corr", [P, TT * H], F32))
        stage, corr_done = (ctx.enter_context(nc.semaphore(n)) for n in ("den_stage", "corr_done"))
        block = ctx.enter_context(nc.Block())

        def halves(t):
            return [t[:, h * TT * H // 2:(h + 1) * TT * H // 2] for h in range(2)]

        @block.scalar
        def _(act):
            for h, part in enumerate(halves(corr)):
                act.wait_ge(stage, h + 1)
                act.activation(part, part, ACT.Exp, scale=SCALE0).then_inc(corr_done, 1)
            act.wait_ge(weights_loaded, 16 * n_loads)

        @block.vector
        def _(dve):
            first, last, sums = (halves(t.rearrange("p t h -> p (t h)"))
                                 for t in (m_first[:, :, :], m_all[:, :, :], o_raw[:, :, :, HD]))
            for h in range(2):
                dve.tensor_tensor(halves(corr)[h], first[h], last[h], ALU.subtract).then_inc(stage, 1)
            for h in range(2):
                dve.wait_ge(corr_done, h + 1)
                dve.scalar_tensor_tensor(halves(denom)[h], halves(corr)[h], 1.0, sums[h], ALU.add, ALU.mult).then_inc(stage, 1)


QT = CH // P


def norm_apply(dve, src, stats, moments, rstd, dst, sems, count, tiles=QT):
    dve.wait_ge(sems["rstd"], count + 1)
    for j in range(tiles):
        op = dve.tensor_scalar(dst(j), src[:, j, :], moments[:, j, 0:1], rstd[:, j:j + 1], ALU.subtract, ALU.mult)
    return op


def norm_stats(dve, src, stats, moments, sems, count, tiles=QT):
    for j in range(tiles):
        dve.bn_stats(stats[:, j, :], src[:, j, :]).then_inc(sems["stats"], 1)
    dve.wait_ge(sems["stats"], count * tiles + tiles)
    dve.memset(moments[:, tiles, 0:1], 0.0)
    for j in range(tiles):
        dve.bn_aggr(moments[:, j, :], stats[:, j, :]).then_inc(sems["moments"], 1)


def norm_rstd(pool, moments, var_eps, rstd, eps, half, sems, count, tiles=QT):
    pool.wait_ge(sems["moments"], count * tiles + tiles)
    wait(pool, sems["used"], count)
    pool.tensor_tensor(var_eps[:, :], moments[:, 0:tiles, 1], eps[:, :], ALU.add).then_inc(sems["var"], 1)
    pool.wait_ge(sems["var"], count + 1)
    pool.tensor_tensor(rstd[:, :], var_eps[:, :], half[:, :], ALU.pow).then_inc(sems["rstd"], 1)


def gated_mlp(nc, ident, t, W, o_raw, denom, X):
    with ExitStack() as ctx:
        def sb(name, shape, dt=F32):
            return ctx.enter_context(nc.sbuf_tensor(name, shape, dt))

        def sem(name):
            return ctx.enter_context(nc.semaphore(name))

        wo, w1, w2, h1, h2, w3, s3, bias = (W[n] for n in ("wo", "w1", "w2", "h1", "h2", "w3", "s3", "bias"))
        scales = {n: W[n] for n in ("s1", "s2", "g1", "g2")}
        x_in = [sb(f"x_in{i}", [P, QT, D]) for i in range(2)]
        xb, oc, pre = sb("xb", [P, QT, D]), sb("oc", [P, QT, D]), sb("pre", [P, QT, D])
        x1 = [sb(f"x1_{i}", [P, QT, D]) for i in range(2)]
        oT, x1T = sb("oT_c", [P, CH]), sb("x1T", [P, CH])
        silu = sb("silu", [P, 2, CH])
        gated, hid1, hid2 = (sb(n, [P, MC, CH]) for n in ("gated", "hid1", "hid2"))
        post = sb("post", [P, QT, D])
        const = {n: sb(f"c_{n}", [P, QT]) for n in ("eps", "half")}
        ln = {k: dict(stats=sb(f"stats_{k}", [P, QT, 6]), moments=sb(f"moments_{k}", [P, QT + 1, 2]),
                      var=sb(f"var_{k}", [P, QT]), rstd=sb(f"rstd_{k}", [P, QT]),
                      sems={n: sem(f"{k}_{n}") for n in ("stats", "moments", "var", "rstd", "used")})
              for k in ("front", "back")}
        ring = [ctx.enter_context(nc.psum_tensor(f"ring{i}", [P, CH], F32)) for i in range(4)]
        turn, proj, down = (ctx.enter_context(nc.psum_tensor(n, [P, CH], F32)) for n in ("turn_c", "proj_c", "down_c"))

        const_set, inverted = sem("const_set"), sem("inverted")
        x_loaded = [sem(f"x_in_loaded{i}") for i in range(2)]
        xb_done, oc_done, o_turned, oT_done, projected = (sem(n) for n in ("xb_done", "oc_done", "o_turned2", "oT_done", "projected2"))
        pre_done, x1_done, x1_turned, x1T_done = (sem(n) for n in ("pre_done", "x1_done", "x1_turned", "x1T_done"))
        ab_done, silu_done, gated_done, hid_done, gelu_done = (sem(n) for n in ("ab_done", "silu_done", "gated_done", "hid_done", "gelu_done"))
        down_done, scaled, post_done, x2_done = (sem(n) for n in ("down_done", "scaled", "post_done", "x2_done"))
        block = ctx.enter_context(nc.Block())
        N = B * 2

        def each_pair(eng, body):
            body(0, True, False)
            with eng.Fori(1, B - 1) as b:
                body(b, False, False)
            body(B - 1, False, True)

        @block.sync
        def _(sp):
            def load_x(c, par):
                wait(sp, xb_done, c - 1)
                sp.dma_start(x_in[par][:, :, :],
                             t["x"].rearrange("b (t p) d -> p (b t) d", p=P)[:, bass.ds(c * QT, QT), :]
                             ).then_inc(x_loaded[par], 16)

            load_x(0, 0)
            load_x(1, 1)

            def pair(b, first, last):
                if not last:
                    for i in range(2):
                        load_x(b * 2 + (2 + i), i)

            each_pair(sp, pair)

        @block.gpsimd
        def _(pool):
            pool.memset(const["eps"][:, :], LN_EPS).then_inc(const_set, 1)
            pool.memset(const["half"][:, :], -0.5).then_inc(const_set, 1)
            pool.wait_ge(const_set, 2)

            def rstd(k, c):
                s = ln[k]
                norm_rstd(pool, s["moments"], s["var"], s["rstd"], const["eps"], const["half"], s["sems"], c)

            def add_bias(c, par, b):
                pool.wait_ge(x_loaded[par], b * 16 + 16)
                wait(pool, pre_done, c)
                pool.tensor_tensor(xb[:, :, :], x_in[par][:, :, :],
                                   bias[:, :].unsqueeze(1).to_broadcast([P, QT, D]), ALU.add).then_inc(xb_done, 1)

            add_bias(0, 0, 0)
            rstd("front", 0)

            def pair(b, first, last):
                for i in range(2):
                    c = b * 2 + i
                    if not (last and i == 1):
                        add_bias(c + 1, (i + 1) % 2, b + (i + 1) // 2)
                    if not (first and i == 0):
                        rstd("back", c - 1)
                    if not (last and i == 1):
                        rstd("front", c + 1)

            each_pair(pool, pair)
            rstd("back", N - 1)

        @block.vector
        def _(dve):
            def divide(c):
                wait(dve, o_turned, c)
                own = denom[:, bass.ds(c * (QT * H), QT * H)]
                dve.reciprocal(own, own).then_inc(inverted, 1)
                dve.wait_ge(inverted, c + 1)
                dve.tensor_tensor(oc[:, :, :].rearrange("p t (h d) -> p (t h) d", d=HD),
                                  o_raw[:, bass.ds(c * QT, QT), :, 0:HD].rearrange("p t h d -> p (t h) d"),
                                  own.unsqueeze(2).to_broadcast([P, QT * H, HD]),
                                  ALU.mult).then_inc(oc_done, 1)

            def front(c, par):
                dve.wait_ge(projected, c + 1)
                dve.wait_ge(xb_done, c + 1)
                wait(dve, x1_done, c)
                dve.tensor_tensor(pre[:, :, :], proj[:, :].rearrange("p (t d) -> p t d", d=D), xb[:, :, :],
                                  ALU.add).then_inc(pre_done, 1)
                dve.wait_ge(pre_done, c + 1)
                s = ln["front"]
                norm_stats(dve, pre, s["stats"], s["moments"], s["sems"], c)
                wait(dve, post_done, c - 1)
                op = norm_apply(dve, pre, s["stats"], s["moments"], s["rstd"], lambda j: x1[par][:, j, :], s["sems"], c)
                op.then_inc(x1_done, 1)
                dve.wait_ge(x1_done, c + 1)
                dve.sem_inc(s["sems"]["used"], 1)

            def gate(c):
                for m in range(MC):
                    dve.wait_ge(silu_done, c * MC + (m + 1))
                    dve.wait_ge(ab_done, c * (2 * MC) + (2 * m + 2))
                    if m == 0:
                        wait(dve, hid_done, c * (2 * MC) - MC)
                    dve.scalar_tensor_tensor(gated[:, m, :], ring[(2 * m + 1) % 4][:, :], scales["s2"][:, m:m + 1],
                                             silu[:, m % 2, :], ALU.mult, ALU.mult).then_inc(gated_done, 1)

            def back(c, par):
                dve.wait_ge(down_done, c + 1)
                wait(dve, x2_done, c)
                dve.tensor_tensor(post[:, :, :], down[:, :].rearrange("p (t d) -> p t d", d=D),
                                  s3[:, :].unsqueeze(1).to_broadcast([P, QT, D]), ALU.mult).then_inc(scaled, 1)
                dve.wait_ge(scaled, c + 1)
                dve.tensor_tensor(post[:, :, :], post[:, :, :], x1[par][:, :, :], ALU.add).then_inc(post_done, 1)
                dve.wait_ge(post_done, c + 1)
                s = ln["back"]
                norm_stats(dve, post, s["stats"], s["moments"], s["sems"], c)
                op = norm_apply(dve, post, s["stats"], s["moments"], s["rstd"],
                                lambda j: X[:, bass.ds(c * QT + j, 1), :].rearrange("p a d -> p (a d)"), s["sems"], c)
                op.then_inc(x2_done, 1)
                dve.wait_ge(x2_done, c + 1)
                dve.sem_inc(s["sems"]["used"], 1)

            divide(0)
            front(0, 0)
            divide(1)

            def pair(b, first, last):
                for i in range(2):
                    c = b * 2 + i
                    gate(c)
                    if not (first and i == 0):
                        back(c - 1, 1 - i)
                    if not (last and i == 1):
                        front(c + 1, (i + 1) % 2)
                    if not last:
                        divide(c + 2)

            each_pair(dve, pair)
            back(N - 1, 1)

        @block.scalar
        def _(act):
            def copy_oT(c):
                act.wait_ge(o_turned, c + 1)
                wait(act, projected, c)
                act.activation(oT[:, :], turn[:, :], ACT.Copy).then_inc(oT_done, 1)

            def copy_x1T(c):
                act.wait_ge(x1_turned, c + 1)
                wait(act, ab_done, c * (2 * MC))
                act.activation(x1T[:, :], turn[:, :], ACT.Copy).then_inc(x1T_done, 1)

            def gelu(c, n, dst, scale, m):
                act.wait_ge(hid_done, c * (2 * MC) + (n + 1))
                act.activation(dst[:, m, :], ring[n % 4][:, :], ACT.Gelu, scale=scale[:, m:m + 1]).then_inc(gelu_done, 1)

            copy_oT(0)
            copy_x1T(0)

            def pair(b, first, last):
                for i in range(2):
                    c = b * 2 + i
                    for m in range(MC):
                        act.wait_ge(ab_done, c * (2 * MC) + (2 * m + 1))
                        wait(act, gated_done, c * MC + (m - 1))
                        act.activation(silu[:, m % 2, :], ring[2 * m % 4][:, :], ACT.Silu,
                                       scale=scales["s1"][:, m:m + 1]).then_inc(silu_done, 1)
                    if not (last and i == 1):
                        copy_oT(c + 1)
                    for m in range(MC):
                        if m == 0:
                            wait(act, hid_done, c * (2 * MC))
                        gelu(c, m, hid1, scales["g1"], m)
                    for m in range(MC):
                        if m == 0:
                            wait(act, down_done, c)
                        if m == 2 and not (last and i == 1):
                            copy_x1T(c + 1)
                        gelu(c, MC + m, hid2, scales["g2"], m)

            each_pair(act, pair)

        @block.tensor
        def _(pe):
            def turn_o(c):
                pe.wait_ge(oc_done, c + 1)
                wait(pe, x1T_done, c)
                for j in range(QT):
                    mm = pe.transpose(turn[:, j * P:(j + 1) * P], oc[:, j, :], ident[:, :])
                mm.then_inc(o_turned, 1)

            def project(c):
                pe.wait_ge(oT_done, c + 1)
                wait(pe, pre_done, c)
                for j in range(QT):
                    mm = pe.matmul(proj[:, j * D:(j + 1) * D], oT[:, j * P:(j + 1) * P], wo[:, :], start=True, stop=True)
                mm.then_inc(projected, 1)

            def turn_x1(c, par):
                pe.wait_ge(x1_done, c + 1)
                pe.wait_ge(oT_done, c + 1)
                for j in range(QT):
                    mm = pe.transpose(turn[:, j * P:(j + 1) * P], x1[par][:, j, :], ident[:, :])
                mm.then_inc(x1_turned, 1)

            def gates(c, tiles):
                pe.wait_ge(x1T_done, c + 1)
                for m in tiles:
                    for o, w in enumerate((w1, w2)):
                        if m < 2:
                            wait(pe, gelu_done, c * (2 * MC) + (2 * m + o - MC + 1))
                        elif o == 0:
                            pe.wait_ge(silu_done, c * MC + (m - 1))
                        else:
                            pe.wait_ge(gated_done, c * MC + (m - 1))
                        pe.matmul(ring[(2 * m + o) % 4][:, :], w[:, m * P:(m + 1) * P], x1T[:, :], start=True,
                                  stop=True).then_inc(ab_done, 1)

            def hidden(c, n, w, src, m):
                if n < 4 and n % 2 == 0:
                    pe.wait_ge(silu_done, c * MC + (3 + n // 2))
                elif n < 4:
                    pe.wait_ge(gated_done, c * MC + (3 + n // 2))
                else:
                    pe.wait_ge(gelu_done, c * (2 * MC) + (n - 3))
                for k in range(MC):
                    if n == 0:
                        pe.wait_ge(gated_done, c * MC + (k + 1))
                    if n == MC:
                        pe.wait_ge(gelu_done, c * (2 * MC) + (k + 1))
                    mm = pe.matmul(ring[n % 4][:, :], w[:, k, m * P:(m + 1) * P], src[:, k, :], start=(k == 0),
                                   stop=(k == MC - 1))
                mm.then_inc(hid_done, 1)

            def downward(c):
                wait(pe, scaled, c)
                pe.wait_ge(gelu_done, c * (2 * MC) + 2 * MC)
                for j in range(QT):
                    for k in range(MC):
                        mm = pe.matmul(down[:, j * D:(j + 1) * D], hid2[:, k, j * P:(j + 1) * P], w3[:, k, :],
                                       start=(k == 0), stop=(k == MC - 1))
                mm.then_inc(down_done, 1)

            turn_o(0)
            project(0)
            turn_x1(0, 0)
            gates(0, (0, 1))

            def pair(b, first, last):
                for i in range(2):
                    c = b * 2 + i
                    ahead = not (last and i == 1)
                    gates(c, (2, 3))
                    if ahead:
                        turn_o(c + 1)
                    for m in range(MC):
                        if m == 2 and ahead:
                            project(c + 1)
                        hidden(c, m, h1, gated, m)
                    for m in range(MC):
                        if m == 2 and ahead:
                            turn_x1(c + 1, (i + 1) % 2)
                        hidden(c, MC + m, h2, hid1, m)
                    if ahead:
                        gates(c + 1, (0, 1))
                    downward(c)

            each_pair(pe, pair)


def causal_attention(nc, ident, W, X):
    with ExitStack() as ctx:
        def sb(name, shape, dt=F32):
            return ctx.enter_context(nc.sbuf_tensor(name, shape, dt))

        def sem(name):
            return ctx.enter_context(nc.semaphore(name))

        def ps(name, cols=CH):
            return ctx.enter_context(nc.psum_tensor(name, [P, cols], F32))

        SC = float(D) ** -0.5
        PIECES = 6
        TURNS = sum((i // QT) + 1 for i in range(NT))
        qk, ov, mask = W["qk"], W["ov"], sb("mask", [P, P])
        xs = [sb(f"xs{i}", [P, NT, D]) for i in range(2)]
        xT = [sb(f"xT{i}", [P, S]) for i in range(2)]
        yT = [sb(f"yT{i}", [P, S]) for i in range(2)]
        xov = [sb(f"xov{i}", [P, NT, D]) for i in range(2)]
        prob = [sb(f"prob_d{i}", [P, S]) for i in range(2)]
        pT = [sb(f"pT{i}", [P, NT, P]) for i in range(2)]
        top, neg, inv = (sb(n, [P, 2]) for n in ("row_top", "row_neg", "row_inv"))
        total = sb("row_total", [P, 4])
        pre = sb("pre_d", [P, QT, D])
        eps, half = sb("eps_d", [P, QT]), sb("half_d", [P, QT])
        stats, moments, var, rstd = sb("stats_d", [P, QT, 6]), sb("moments_d", [P, QT + 1, 2]), sb("var_d", [P, QT]), sb("rstd_d", [P, QT])
        sems = {n: sem(f"d_{n}") for n in ("stats", "moments", "var", "rstd", "used")}
        score = [ps(f"score{i}", 2 * CH) for i in range(2)]
        turned, piece, outp = [ps(f"turned{i}") for i in range(2)], ps("piece"), ps("outp")
        const_set, mask_set = sem("const_set_d"), sem("mask_set")
        xs_done, made, copied = sem("xs_done"), sem("piece_made"), sem("piece_copied")
        scored, masked, topped, negged, exp_done = (sem(n) for n in ("scored_d", "masked", "topped", "negged", "exp_done_d"))
        turn_done, turn_copied, pv_done, inv_done, pre_done, x_done = (sem(n) for n in ("turn_done", "turn_copied", "pv_done_d", "inv_done", "pre_done_d", "x_done"))
        block = ctx.enter_context(nc.Block())

        def turns_to(i):
            return sum((k // QT) + 1 for k in range(i + 1)) if i >= 0 else -sum((NT + k) // QT + 1 for k in range(i + 1, 0))

        def each_pair(eng, body):
            body(0, True, False)
            with eng.Fori(1, B // 2 - 1) as b:
                body(b, False, False)
            body(B // 2 - 1, False, True)

        @block.gpsimd
        def _(pool):
            pool.memset(mask[:, :], 0.0).then_inc(const_set, 1)
            pool.memset(eps[:, :], LN_EPS).then_inc(const_set, 1)
            pool.memset(half[:, :], -0.5).then_inc(const_set, 1)
            pool.wait_ge(const_set, 3)
            pool.affine_select(out=mask[:, :], in_=mask[:, :], compare_op=ALU.is_ge, fill=-1e30, base=0,
                               pattern=[[-1, P]], channel_multiplier=1).then_inc(mask_set, 1)

            def pair(b, first, last):
                for i in range(4):
                    norm_rstd(pool, moments, var, rstd, eps, half, sems, b * 4 + i)

            each_pair(pool, pair)

        @block.scalar
        def _(act):
            def take_x(bb, par):
                wait(act, pre_done, bb * NT - NT)
                act.activation(xs[par][:, :, :], X[:, bass.ds(bb * NT, NT), :], ACT.Copy).then_inc(xs_done, 1)

            def exps(bb, i):
                n = bb * NT + i
                act.wait_ge(negged, n + 1)
                wait(act, turn_done, bb * TURNS + turns_to(i - 2))
                wait(act, pre_done, n - 3)
                act.activation(prob[i % 2][:, 0:(i + 1) * P], score[i % 2][:, 0:(i + 1) * P], ACT.Exp, scale=SC,
                               bias=neg[:, i % 2:i % 2 + 1], accum_out=total[:, i % 4:i % 4 + 1]).then_inc(exp_done, 1)

            take_x(0, 0)
            exps(0, 0)

            def batch(bb, par, first, last):
                for i in range(NT):
                    if i == 1 and not last:
                        take_x(bb + 1, 1 - par)
                    for p in range(i // QT + 1):
                        k = turns_to(i - 1) + p
                        act.wait_ge(turn_done, bb * TURNS + (k + 1))
                        if p == 0:
                            wait(act, pv_done, bb * NT + (i - 1))
                        n = min(QT, i + 1 - p * QT)
                        act.activation(pT[i % 2][:, p * QT:p * QT + n, :].rearrange("p a b -> p (a b)"),
                                       turned[k % 2][:, 0:n * P], ACT.Copy).then_inc(turn_copied, 1)
                    if not (last and i == NT - 1):
                        exps(bb + (i + 1) // NT, (i + 1) % NT)

            def pair(b, first, last):
                for i in range(2):
                    batch(b * 2 + i, i, first and i == 0, last and i == 1)

            each_pair(act, pair)

        @block.vector
        def _(dve):
            def softmax_top(bb, i):
                n = bb * NT + i
                dve.wait_ge(scored, n + 1)
                diag = score[i % 2][:, i * P:(i + 1) * P]
                dve.tensor_tensor(diag, diag, mask[:, :], ALU.add).then_inc(masked, 1)
                dve.wait_ge(masked, n + 1)
                dve.tensor_reduce(top[:, i % 2:i % 2 + 1], score[i % 2][:, 0:(i + 1) * P], AX_X, ALU.max).then_inc(topped, 1)
                dve.wait_ge(topped, n + 1)
                wait(dve, exp_done, n - 1)
                dve.tensor_scalar(neg[:, i % 2:i % 2 + 1], top[:, i % 2:i % 2 + 1], -SC, None, ALU.mult).then_inc(negged, 1)

            def copy_piece(bb, f, par):
                dve.wait_ge(made, bb * PIECES + (f + 1))
                if f == 0:
                    wait(dve, scored, bb * NT - NT)
                if f == 4:
                    wait(dve, pv_done, bb * NT - NT)
                h = f % 2
                dst = (xT[par][:, h * CH:(h + 1) * CH], yT[par][:, h * CH:(h + 1) * CH],
                       xov[par][:, h * QT:(h + 1) * QT, :].rearrange("p a b -> p (a b)"))[f // 2]
                dve.tensor_copy(dst, piece[:, :]).then_inc(copied, 1)

            def residual(bb, i, par):
                n = bb * NT + i
                dve.wait_ge(exp_done, n + 1)
                dve.reciprocal(inv[:, i % 2:i % 2 + 1], total[:, i % 4:i % 4 + 1]).then_inc(inv_done, 1)
                dve.wait_ge(inv_done, n + 1)
                dve.wait_ge(pv_done, n + 1)
                if i % QT == 0:
                    wait(dve, x_done, bb * 2 + i // QT)
                dve.scalar_tensor_tensor(pre[:, i % QT, :], outp[:, 0:D], inv[:, i % 2:i % 2 + 1], xs[par][:, i, :],
                                         ALU.mult, ALU.add).then_inc(pre_done, 1)
                if i % QT == QT - 1:
                    g = bb * 2 + i // QT
                    dve.wait_ge(pre_done, n + 1)
                    norm_stats(dve, pre, stats, moments, sems, g)

            def finish(g):
                op = norm_apply(dve, pre, stats, moments, rstd,
                                lambda j: X[:, bass.ds(g * QT + j, 1), :].rearrange("p a d -> p (a d)"), sems, g)
                op.then_inc(x_done, 1)
                dve.wait_ge(x_done, g + 1)
                dve.sem_inc(sems["used"], 1)

            for f in range(PIECES):
                copy_piece(0, f, 0)
            dve.wait_ge(mask_set, 1)
            softmax_top(0, 0)

            def batch(bb, par, first, last):
                for i in range(NT):
                    if not (last and i == NT - 1):
                        softmax_top(bb + (i + 1) // NT, (i + 1) % NT)
                    if 1 <= i <= PIECES and not last:
                        copy_piece(bb + 1, i - 1, 1 - par)
                    if i == QT + 1:
                        finish(bb * 2)
                    elif i == 1 and not first:
                        finish(bb * 2 - 1)
                    if i >= 1:
                        residual(bb, i - 1, par)
                    elif not first:
                        residual(bb - 1, NT - 1, 1 - par)

            def pair(b, first, last):
                for i in range(2):
                    batch(b * 2 + i, i, first and i == 0, last and i == 1)

            each_pair(dve, pair)
            residual(B - 1, NT - 1, 1)
            finish(B * 2 - 1)

        @block.tensor
        def _(pe):
            def make_piece(bb, f, par):
                if f == 0:
                    pe.wait_ge(xs_done, bb + 1)
                wait(pe, copied, bb * PIECES + f)
                h = f % 2
                if f // 2 == 1:
                    mm = pe.matmul(piece[:, :], qk[:, :], xT[par][:, h * CH:(h + 1) * CH], start=True, stop=True)
                else:
                    for j in range(QT):
                        dst = piece[:, j * P:(j + 1) * P]
                        if f // 2 == 0:
                            mm = pe.transpose(dst, xs[par][:, h * QT + j, :], ident[:, :])
                        else:
                            mm = pe.matmul(dst, xT[par][:, (h * QT + j) * P:(h * QT + j + 1) * P], ov[:, :],
                                           start=True, stop=True)
                mm.then_inc(made, 1)

            def scores(bb, i, par):
                if i == 0:
                    pe.wait_ge(copied, bb * PIECES + 4)
                wait(pe, exp_done, bb * NT + (i - 1))
                for k in range(i // QT + 1):
                    w = min(CH, (i + 1) * P - k * CH)
                    mm = pe.matmul(score[i % 2][:, k * CH:k * CH + w], yT[par][:, i * P:(i + 1) * P],
                                   xT[par][:, k * CH:k * CH + w], start=True, stop=True)
                mm.then_inc(scored, 1)

            def turn_probs(bb, i):
                pe.wait_ge(exp_done, bb * NT + (i + 1))
                for p in range(i // QT + 1):
                    k = turns_to(i - 1) + p
                    wait(pe, turn_copied, bb * TURNS + (k - 1))
                    for j in range(min(QT, i + 1 - p * QT)):
                        mm = pe.transpose(turned[k % 2][:, j * P:(j + 1) * P],
                                          prob[i % 2][:, (p * QT + j) * P:(p * QT + j + 1) * P], ident[:, :])
                    mm.then_inc(turn_done, 1)

            def values(bb, i, par):
                pe.wait_ge(turn_copied, bb * TURNS + turns_to(i))
                wait(pe, pre_done, bb * NT + i)
                if i == 0:
                    pe.wait_ge(copied, bb * PIECES + PIECES)
                for j in range(i + 1):
                    mm = pe.matmul(outp[:, 0:D], pT[i % 2][:, j, :], xov[par][:, j, :], start=(j == 0), stop=(j == i))
                mm.then_inc(pv_done, 1)

            for f in range(PIECES):
                make_piece(0, f, 0)
            scores(0, 0, 0)

            def batch(bb, par, first, last):
                for i in range(NT):
                    if i < NT - 1:
                        scores(bb, i + 1, par)
                    elif not last:
                        scores(bb + 1, 0, 1 - par)
                    if 1 <= i <= PIECES and not last:
                        make_piece(bb + 1, i - 1, 1 - par)
                    if i >= 1:
                        values(bb, i - 1, par)
                    elif not first:
                        values(bb - 1, NT - 1, 1 - par)
                    turn_probs(bb, i)

            def pair(b, first, last):
                for i in range(2):
                    batch(b * 2 + i, i, first and i == 0, last and i == 1)

            each_pair(pe, pair)
            values(B - 1, NT - 1, 1)


def soft_experts(nc, ident, W, X, out):
    with ExitStack() as ctx:
        def sb(name, shape, dt=F32):
            return ctx.enter_context(nc.sbuf_tensor(name, shape, dt))

        def sem(name):
            return ctx.enter_context(nc.semaphore(name))

        def ps(name, cols=CH):
            return ctx.enter_context(nc.psum_tensor(name, [P, cols], F32))

        NE, NS, EH = 16, 16, 32
        SL = NE * NS
        EG = P // EH
        GR = NE // EG
        GS = EG * NS
        TINY = 1e-24

        mu, gamma, beta, scale, ew1, ew2, b1, b2 = (W[n] for n in ("mu", "gamma", "beta", "mscale", "ew1", "ew2", "eb1", "eb2"))
        mu_sq, mu_unit = sb("mu_sq", [P, SL]), sb("mu_unit", [P, SL])
        mu_sum, mu_inv, mu_diag = sb("mu_sum", [P, 2]), sb("mu_inv", [P, 2]), sb("mu_diag", [P, 2, P])
        ones = sb("ones_e", [P, P])
        own = sb("own", [P, GR, GS])
        eps, half = sb("eps_e", [P, NT]), sb("half_e", [P, NT])
        xm, xg, sq, xu = (sb(n, [P, NT, D]) for n in ("xm", "xg", "sq", "xu"))
        xn = [sb(f"xn{i}", [P, NT, D]) for i in range(2)]
        f_stats, f_moments, f_var, f_rstd = sb("f_stats", [P, NT, 6]), sb("f_moments", [P, NT + 1, 2]), sb("f_var", [P, NT]), sb("f_rstd", [P, NT])
        sumsq, guarded, inv_norm = (sb(n, [P, NT]) for n in ("sumsq", "guarded", "inv_norm"))
        xuT, comb = sb("xuT", [P, S]), sb("comb", [P, NT, SL])
        row_top, row_neg = sb("row_top_e", [P, NT]), sb("row_neg_e", [P, NT])
        row_sum, row_inv = [sb(f"row_sum{i}", [P, NT]) for i in range(2)], [sb(f"row_inv{i}", [P, NT]) for i in range(2)]
        combT = [sb(f"combT{i}", [P, 2, S]) for i in range(2)]
        dispT, disp = sb("dispT", [P, 2, S]), sb("disp", [P, NT, SL])
        col_top, col_neg, col_sum, col_inv = (sb(n, [P, 2]) for n in ("col_top", "col_neg", "col_sum", "col_inv"))
        slotT, act_h, own_h, slot_out = sb("slotT", [P, SL]), sb("act_h", [P, GR, GS]), sb("own_h", [P, GR, GS]), sb("slot_out", [P, 2, D])
        pre = sb("pre_e", [P, NT, D])
        fin = [sb(f"fin{i}", [P, NT, D]) for i in range(2)]
        l_stats, l_moments, l_var, l_rstd = sb("l_stats", [P, NT, 6]), sb("l_moments", [P, NT + 1, 2]), sb("l_var", [P, NT]), sb("l_rstd", [P, NT])

        ring, colp = [ps(f"ring_e{i}") for i in range(2)], ps("colp", 2 * CH)
        slot_hid, so_ps, out_ps = ps("slot_hid"), ps("so_ps"), ps("out_ps", 2 * CH)
        slot_ps, hid_ps = slot_hid[:, 0:SL], slot_hid[:, SL:2 * SL]
        fs = {n: sem(f"f_{n}") for n in ("stats", "moments", "var", "rstd", "used")}
        ls = {n: sem(f"l_{n}") for n in ("stats", "moments", "var", "rstd", "used")}
        const_set, mu_step, own_set = sem("const_set_e"), sem("mu_step"), sem("own_set")
        xm_done, xg_done, xn_done, sq_done, sumsq_done, guard_done, inorm_done, xu_done = (sem(n) for n in (
            "xm_done", "xg_done", "xn_done", "sq_done", "sumsq_done", "guard_done", "inorm_done", "xu_done"))
        ring_ready, ring_free = [sem(f"ring_ready{i}") for i in range(2)], [sem(f"ring_free{i}") for i in range(2)]
        row_topped, row_negged, row_exp, row_inved = sem("row_topped"), sem("row_negged"), sem("row_exp"), sem("row_inved")
        col_scored, col_topped, col_negged, col_exp, col_inved, disp_normed = (sem(n) for n in (
            "col_scored", "col_topped", "col_negged", "col_exp", "col_inved", "disp_normed"))
        slotted, slot_copied, hidden_done, gelu_done, owned, so_done, so_added = (sem(n) for n in (
            "slotted", "slot_copied", "hidden_done", "gelu_done_e", "owned", "so_done", "so_added"))
        combined, added, fin_done, stored = sem("combined"), sem("added"), sem("fin_done"), [sem(f"stored{i}") for i in range(2)]
        block = ctx.enter_context(nc.Block())

        FRONT = ["xT0", "xT1", "rl0", "rl1", "rl2", "rl3", "cT0", "cT1", "cT2", "cT3"]
        BOTH = ["xT0", "xT1", "dT0", "dT1", "rl0", "rl1", "dT2", "dT3", "rl2", "rl3", "cT0", "cT1", "cT2", "cT3"]
        BACK = ["dT0", "dT1", "dT2", "dT3"]

        def task(name, b):
            tasks, before = (FRONT, 0) if b is None else (BACK if isinstance(b, int) and b == B - 1 else BOTH, None)
            k = tasks.index(name)
            if before is None:
                before = b * (len(BOTH) // 2) + len(FRONT) // 2
            return k % 2, before + k // 2

        def each_pair(eng, body):
            body(0, True, False)
            with eng.Fori(1, B // 2 - 1) as b:
                body(b, False, False)
            body(B // 2 - 1, False, True)

        def wide(v):
            return v[:, :].unsqueeze(1).to_broadcast([P, NT, D])

        def affine(eng, b, par):
            eng.wait_ge(xm_done, b + 1)
            eng.tensor_tensor(xg[:, :, :], xm[:, :, :], wide(gamma), ALU.mult).then_inc(xg_done, 1)
            eng.wait_ge(xg_done, b + 1)
            wait(eng, slotted, b - 1)
            eng.tensor_tensor(xn[par][:, :, :], xg[:, :, :], wide(beta), ALU.add).then_inc(xn_done, 1)
            eng.wait_ge(xn_done, b + 1)
            wait(eng, sumsq_done, b)
            eng.tensor_tensor(sq[:, :, :], xn[par][:, :, :], xn[par][:, :, :], ALU.mult).then_inc(sq_done, 1)

        def steps(eng, step):
            def pair(b, first, last):
                for i in range(2):
                    step(b * 2 + i, i, first and i == 0, last and i == 1, last)
            each_pair(eng, pair)

        @block.sync
        def _(sp):
            def step(b, par, first, last, last_pair):
                sp.wait_ge(fin_done, b + 1)
                sp.dma_start(out.rearrange("b (t p) d -> p (b t) d", p=P)[:, bass.ds(b * NT, NT), :],
                             fin[par][:, :, :]).then_inc(stored[par], 16)

            steps(sp, step)
            for i in range(2):
                sp.wait_ge(stored[i], B // 2 * 16)

        @block.gpsimd
        def _(pool):
            pool.memset(eps[:, :], LN_EPS).then_inc(const_set, 1)
            pool.memset(half[:, :], -0.5).then_inc(const_set, 1)
            pool.memset(ones[:, :], 1.0).then_inc(const_set, 1)
            pool.wait_ge(const_set, 3)
            pool.tensor_tensor(mu_sq[:, :], mu[:, :], mu[:, :], ALU.mult).then_inc(mu_step, 1)

            def norm(b):
                pool.wait_ge(fs["moments"], b * NT + NT)
                pool.tensor_tensor(f_var[:, :], f_moments[:, 0:NT, 1], eps[:, :], ALU.add).then_inc(fs["var"], 1)
                pool.wait_ge(fs["var"], b + 1)
                wait(pool, xm_done, b)
                pool.tensor_tensor(f_rstd[:, :], f_var[:, :], half[:, :], ALU.pow).then_inc(fs["rstd"], 1)

            def invert_norm(b):
                pool.wait_ge(guard_done, b + 1)
                wait(pool, xu_done, b)
                pool.tensor_tensor(inv_norm[:, :], guarded[:, :], half[:, :], ALU.pow).then_inc(inorm_done, 1)

            pool.wait_ge(mu_step, 3)
            pool.tensor_tensor(mu_inv[:, :], mu_sum[:, :], half[:, 0:2], ALU.pow).then_inc(mu_step, 1)
            norm(0)
            invert_norm(0)
            norm(1)
            affine(pool, 1, 1)
            invert_norm(1)

            def step(b, par, first, last, last_pair):
                if not last_pair:
                    norm(b + 2)
                    affine(pool, b + 2, par)
                    invert_norm(b + 2)
                if not first:
                    norm_rstd(pool, l_moments, l_var, l_rstd, eps, half, ls, b - 1, NT)

            steps(pool, step)
            norm_rstd(pool, l_moments, l_var, l_rstd, eps, half, ls, B - 1, NT)

        @block.vector
        def _(dve):
            def norm_tokens_stats(b):
                for j in range(NT):
                    dve.bn_stats(f_stats[:, j, :], X[:, bass.ds(b * NT + j, 1), :].rearrange("p a d -> p (a d)")).then_inc(fs["stats"], 1)
                dve.wait_ge(fs["stats"], b * NT + NT)
                dve.memset(f_moments[:, NT, 0:1], 0.0)
                for j in range(NT):
                    dve.bn_aggr(f_moments[:, j, :], f_stats[:, j, :]).then_inc(fs["moments"], 1)

            def norm_tokens(b):
                dve.wait_ge(fs["rstd"], b + 1)
                wait(dve, xg_done, b)
                for j in range(NT):
                    op = dve.tensor_scalar(xm[:, j, :], X[:, bass.ds(b * NT + j, 1), :].rearrange("p a d -> p (a d)"),
                                           f_moments[:, j, 0:1], f_rstd[:, j:j + 1], ALU.subtract, ALU.mult)
                op.then_inc(xm_done, 1)

            def guard_norms(b):
                dve.wait_ge(sq_done, b + 1)
                dve.tensor_reduce(sumsq[:, :], sq[:, :, :], AX_X, ALU.add).then_inc(sumsq_done, 1)
                dve.wait_ge(sumsq_done, b + 1)
                wait(dve, inorm_done, b)
                dve.tensor_scalar(guarded[:, :], sumsq[:, :], TINY, None, ALU.max).then_inc(guard_done, 1)

            def unit(b, par, before):
                dve.wait_ge(inorm_done, b + 1)
                wait(dve, ring_ready[1], before)
                dve.tensor_tensor(xu[:, :, :], xn[par][:, :, :], inv_norm[:, :].unsqueeze(2).to_broadcast([P, NT, D]),
                                  ALU.mult).then_inc(xu_done, 1)

            def ring_wait(eng, name, s):
                i, before = task(name, s)
                eng.wait_ge(ring_ready[i], before + 1)
                return i

            def row_max(b, s, q):
                i = ring_wait(dve, f"rl{q}", s)
                wait(dve, row_negged, b * 4 + q)
                dve.tensor_reduce(row_top[:, 2 * q:2 * q + 2], ring[i][:, :].rearrange("p (t s) -> p t s", s=SL), AX_X,
                                  ALU.max).then_inc(row_topped, 1)
                dve.wait_ge(row_topped, b * 4 + (q + 1))
                if q == 0:
                    wait(dve, row_exp, b * NT)
                dve.tensor_scalar(row_neg[:, 2 * q:2 * q + 2], row_top[:, 2 * q:2 * q + 2], -1.0, None,
                                  ALU.mult).then_inc(row_negged, 1)

            def col_max(b, h):
                dve.wait_ge(col_scored, b * 2 + (h + 1))
                dve.tensor_reduce(col_top[:, h:h + 1], colp[:, :], AX_X, ALU.max).then_inc(col_topped, 1)
                dve.wait_ge(col_topped, b * 2 + (h + 1))
                dve.tensor_scalar(col_neg[:, h:h + 1], col_top[:, h:h + 1], -1.0, None, ALU.mult).then_inc(col_negged, 1)

            def col_norm(b, h):
                dve.wait_ge(col_exp, b * 2 + (h + 1))
                dve.reciprocal(col_inv[:, h:h + 1], col_sum[:, h:h + 1]).then_inc(col_inved, 1)
                dve.wait_ge(col_inved, b * 2 + (h + 1))
                dve.tensor_scalar(dispT[:, h, :], dispT[:, h, :], col_inv[:, h:h + 1], None, ALU.mult).then_inc(disp_normed, 1)

            def rows_inv(b, par):
                dve.wait_ge(row_exp, b * NT + NT)
                dve.reciprocal(row_inv[par][:, :], row_sum[par][:, :]).then_inc(row_inved, 1)

            def add_combined(b, par):
                dve.wait_ge(combined, b + 1)
                dve.wait_ge(row_inved, b + 1)
                wait(dve, fin_done, b)
                for j in range(NT):
                    op = dve.scalar_tensor_tensor(pre[:, j, :], out_ps[:, j * D:(j + 1) * D], row_inv[par][:, j:j + 1],
                                                  X[:, bass.ds(b * NT + j, 1), :].rearrange("p a d -> p (a d)"),
                                                  ALU.mult, ALU.add)
                op.then_inc(added, 1)

            def output_stats(b):
                dve.wait_ge(added, b + 1)
                norm_stats(dve, pre, l_stats, l_moments, ls, b, NT)

            def output(b, par):
                wait(dve, stored[par], b * 8 - par * 8)
                op = norm_apply(dve, pre, l_stats, l_moments, l_rstd, lambda j: fin[par][:, j, :], ls, b, NT)
                op.then_inc(fin_done, 1)
                dve.wait_ge(fin_done, b + 1)
                dve.sem_inc(ls["used"], 1)

            norm_tokens_stats(0)
            dve.wait_ge(mu_step, 2)
            dve.tensor_scalar(mu_sum[:, :], slot_ps[:, 0:2], TINY, None, ALU.max).then_inc(mu_step, 1)
            dve.wait_ge(mu_step, 4)
            for h in range(2):
                dve.tensor_scalar(mu_diag[:, h, :], ident[:, :], mu_inv[:, h:h + 1], None, ALU.mult).then_inc(mu_step, 1)
            norm_tokens(0)
            affine(dve, 0, 0)
            guard_norms(0)
            norm_tokens_stats(1)
            unit(0, 0, 0)
            dve.wait_ge(mu_step, 7)
            dve.scalar_tensor_tensor(mu_unit[:, :], mu[:, :], scale[:, 0:1], slot_ps[:, :], ALU.mult, ALU.mult).then_inc(mu_step, 1)
            norm_tokens(1)
            dve.memset(own[:, :, :], 0.0).then_inc(own_set, 1)
            dve.wait_ge(own_set, 1)
            for e in range(EG):
                dve.memset(own[e * EH:(e + 1) * EH, :, e * NS:(e + 1) * NS], 1.0).then_inc(own_set, 1)
            for q in range(4):
                row_max(0, None, q)
            guard_norms(1)
            col_max(0, 0)
            col_norm(0, 0)
            unit(1, 1, 1)
            col_max(0, 1)
            col_norm(0, 1)

            def step(b, par, first, last, last_pair):
                ahead = not last_pair
                rows_inv(b, par)
                if not last:
                    row_max(b + 1, b, 0)
                    row_max(b + 1, b, 1)
                if ahead:
                    norm_tokens_stats(b + 2)
                if not last:
                    row_max(b + 1, b, 2)
                    row_max(b + 1, b, 3)
                if ahead:
                    norm_tokens(b + 2)
                dve.wait_ge(slotted, b + 1)
                dve.tensor_copy(slotT[:, :], slot_ps[:, :]).then_inc(slot_copied, 1)
                if not last:
                    col_max(b + 1, 0)
                if not first:
                    add_combined(b - 1, 1 - par)
                dve.wait_ge(gelu_done, b * GR + GR)
                dve.tensor_tensor(own_h[:, :, :], act_h[:, :, :], own[:, :, :], ALU.mult).then_inc(owned, 1)
                if not last:
                    col_norm(b + 1, 0)
                    col_max(b + 1, 1)
                dve.wait_ge(so_done, b + 1)
                dve.tensor_tensor(slot_out[:, :, :], so_ps[:, 0:2 * D].rearrange("p (h d) -> p h d", h=2), b2[:, :, :],
                                  ALU.add).then_inc(so_added, 1)
                if ahead:
                    guard_norms(b + 2)
                if not first:
                    output_stats(b - 1)
                if not last:
                    col_norm(b + 1, 1)
                if ahead:
                    unit(b + 2, par, task("xT1", b)[1] + 1)
                if not first:
                    output(b - 1, 1 - par)

            steps(dve, step)
            add_combined(B - 1, 1)
            output_stats(B - 1)
            output(B - 1, 1)

        @block.scalar
        def _(act):
            def ring_wait(name, s):
                i, before = task(name, s)
                act.wait_ge(ring_ready[i], before + 1)
                return i

            def row_exps(b, par, s, q):
                i, _ = task(f"rl{q}", s)
                act.wait_ge(row_negged, b * 4 + (q + 1))
                if q == 0:
                    i3, before = task("cT3", None if s is None or (isinstance(s, int) and s == 0) else s - 1)
                    if s is not None:
                        act.wait_ge(ring_ready[i3], before + 1)
                    wait(act, row_inved, b - 1)
                for j in range(2):
                    tile = 2 * q + j
                    op = act.activation(comb[:, tile, :], ring[i][:, j * SL:(j + 1) * SL], ACT.Exp,
                                        bias=row_neg[:, tile:tile + 1], accum_out=row_sum[par][:, tile:tile + 1])
                    op.then_inc(row_exp, 1)
                act.wait_ge(row_exp, b * NT + (2 * q + 2))
                act.sem_inc(ring_free[i], 1)

            def copy_x(s):
                for q in range(2):
                    i = ring_wait(f"xT{q}", s)
                    if q == 0 and s is not None:
                        act.wait_ge(col_scored, s * 2 + 2)
                    act.activation(xuT[:, q * CH:(q + 1) * CH], ring[i][:, :], ACT.Copy).then_inc(ring_free[i], 1)

            def col_exps(b, h):
                act.wait_ge(col_negged, b * 2 + (h + 1))
                act.activation(dispT[:, h, :], colp[:, :], ACT.Exp, bias=col_neg[:, h:h + 1],
                               accum_out=col_sum[:, h:h + 1]).then_inc(col_exp, 1)

            def turn_copies(names, dst, s):
                for q in names:
                    i = ring_wait(q, s)
                    act.activation(dst(int(q[2])), ring[i][:, :], ACT.Copy).then_inc(ring_free[i], 1)

            def comb_dst(par):
                return lambda q: combT[par][:, q // 2, (q % 2) * CH:(q % 2 + 1) * CH]

            def disp_dst(q):
                return disp[:, 2 * q:2 * q + 2, :].rearrange("p t s -> p (t s)")

            copy_x(None)
            for q in range(4):
                row_exps(0, 0, None, q)
            turn_copies(["cT0", "cT1"], comb_dst(0), None)
            col_exps(0, 0)
            turn_copies(["cT2", "cT3"], comb_dst(0), None)
            col_exps(0, 1)

            def step(b, par, first, last, last_pair):
                nxt = 1 - par
                if not last:
                    copy_x(b)
                wait(act, slotted, b)
                turn_copies(["dT0", "dT1"], disp_dst, b)
                if not last:
                    row_exps(b + 1, nxt, b, 0)
                    row_exps(b + 1, nxt, b, 1)
                turn_copies(["dT2", "dT3"], disp_dst, b)
                if not last:
                    row_exps(b + 1, nxt, b, 2)
                    row_exps(b + 1, nxt, b, 3)
                    col_exps(b + 1, 0)
                act.wait_ge(hidden_done, b + 1)
                wait(act, owned, b)
                for g in range(GR):
                    act.activation(act_h[:, g, :], hid_ps[:, g * GS:(g + 1) * GS], ACT.Gelu, bias=b1[:, g:g + 1]).then_inc(gelu_done, 1)
                if not last:
                    wait(act, combined, b)
                    turn_copies(["cT0", "cT1"], comb_dst(nxt), b)
                    col_exps(b + 1, 1)
                    turn_copies(["cT2", "cT3"], comb_dst(nxt), b)

            steps(act, step)

        @block.tensor
        def _(pe):
            def fill(name, s, ops):
                i, before = task(name, s)
                wait(pe, ring_free[i], before)
                ops(ring[i]).then_inc(ring_ready[i], 1)

            def turn(src):
                def ops(bank):
                    for j in range(QT):
                        mm = pe.transpose(bank[:, j * P:(j + 1) * P], src(j), ident[:, :])
                    return mm
                return ops

            def turn_x(b, s):
                pe.wait_ge(xu_done, b + 1)
                for q in range(2):
                    fill(f"xT{q}", s, turn(lambda j: xu[:, q * QT + j, :]))

            def row_logits(b, s, qs):
                if qs[0] == 0:
                    for q in range(2):
                        i, before = task(f"xT{q}", s)
                        pe.wait_ge(ring_free[i], before + 1)
                for q in qs:
                    def ops(bank):
                        for j in range(2):
                            tile = 2 * q + j
                            mm = pe.matmul(bank[:, j * SL:(j + 1) * SL], xuT[:, tile * P:(tile + 1) * P], mu_unit[:, :],
                                           start=True, stop=True)
                        return mm
                    fill(f"rl{q}", s, ops)

            def col_logits(b, h):
                wait(pe, col_exp, b * 2 + h)
                for k in range(2):
                    mm = pe.matmul(colp[:, k * CH:(k + 1) * CH], mu_unit[:, h * P:(h + 1) * P], xuT[:, k * CH:(k + 1) * CH],
                                   start=True, stop=True)
                mm.then_inc(col_scored, 1)

            def turn_comb(b, s, qs):
                pe.wait_ge(row_exp, b * NT + NT)
                for q in qs:
                    fill(f"cT{q}", s, turn(lambda j: comb[:, (q % 2) * QT + j, (q // 2) * P:(q // 2 + 1) * P]))

            def turn_disp(b, qs):
                pe.wait_ge(disp_normed, b * 2 + 2)
                for q in qs:
                    fill(f"dT{q}", b, turn(lambda j: dispT[:, j % 2, (2 * q + j // 2) * P:(2 * q + j // 2 + 1) * P]))

            def slots(b, par):
                for q in (2, 3):
                    i, before = task(f"dT{q}", b)
                    pe.wait_ge(ring_free[i], before + 1)
                wait(pe, slot_copied, b)
                for j in range(NT):
                    mm = pe.matmul(slot_ps[:, 0:SL], xn[par][:, j, :], disp[:, j, :], start=(j == 0), stop=(j == NT - 1))
                mm.then_inc(slotted, 1)

            def experts_in(b):
                pe.wait_ge(slot_copied, b + 1)
                wait(pe, gelu_done, b * GR)
                for g in range(GR):
                    mm = pe.matmul(hid_ps[:, g * GS:(g + 1) * GS], ew1[:, g, :], slotT[:, g * GS:(g + 1) * GS], start=True, stop=True)
                mm.then_inc(hidden_done, 1)

            def experts_out(b):
                pe.wait_ge(owned, b + 1)
                wait(pe, so_added, b)
                for g in range(GR):
                    p0 = GS * (g % 2)
                    mm = pe.matmul(so_ps[p0:p0 + GS, (g // 2) * D:(g // 2 + 1) * D], own_h[:, g, :], ew2[:, g, :], start=True, stop=True)
                mm.then_inc(so_done, 1)

            def combine(b, par):
                i, before = task("cT3", None if isinstance(b, int) and b == 0 else b - 1)
                pe.wait_ge(ring_free[i], before + 1)
                pe.wait_ge(so_added, b + 1)
                wait(pe, added, b)
                for j in range(NT):
                    for h in range(2):
                        mm = pe.matmul(out_ps[:, j * D:(j + 1) * D], combT[par][:, h, j * P:(j + 1) * P],
                                       slot_out[:, h, :], start=(h == 0), stop=(h == 1))
                mm.then_inc(combined, 1)

            pe.wait_ge(const_set, 3)
            pe.wait_ge(mu_step, 1)
            for h in range(2):
                mm = pe.matmul(slot_ps[:, h:h + 1], mu_sq[:, h * P:(h + 1) * P], ones[:, 0:1], start=True, stop=True)
            mm.then_inc(mu_step, 1)
            pe.wait_ge(mu_step, 6)
            for h in range(2):
                mm = pe.matmul(slot_ps[:, h * P:(h + 1) * P], ones[:, :], mu_diag[:, h, :], start=True, stop=True)
            mm.then_inc(mu_step, 1)
            turn_x(0, None)
            pe.wait_ge(mu_step, 8)
            row_logits(0, None, (0, 1, 2, 3))
            turn_comb(0, None, (0, 1))
            col_logits(0, 0)
            turn_comb(0, None, (2, 3))
            col_logits(0, 1)

            def step(b, par, first, last, last_pair):
                if not last:
                    turn_x(b + 1, b)
                turn_disp(b, (0, 1))
                if not last:
                    row_logits(b + 1, b, (0, 1))
                turn_disp(b, (2, 3))
                if not last:
                    row_logits(b + 1, b, (2, 3))
                slots(b, par)
                if not last:
                    col_logits(b + 1, 0)
                experts_in(b)
                if not last:
                    turn_comb(b + 1, b, (0, 1))
                    col_logits(b + 1, 1)
                experts_out(b)
                if not last:
                    turn_comb(b + 1, b, (2, 3))
                combine(b, par)

            steps(pe, step)


def weight_tiles(nc, ctx, t, loaded):
    def row(name):
        return t[name].rearrange("(a d) -> a d", a=1)

    W, loads = {}, []

    def tile(name, shape, src, part=None):
        if name not in W:
            W[name] = ctx.enter_context(nc.sbuf_tensor(f"w_{name}", shape, F32))
        dst = W[name][tuple(slice(None) for _ in shape)] if part is None else W[name][:, part, :]
        loads.append((dst, src, loaded))

    tile("wo", [P, D], t["woT"])
    tile("w1", [P, HID], t["w1T"])
    tile("w2", [P, HID], t["w2T"])
    for name, src in (("h1", "h1T"), ("h2", "h2T")):
        tile(name, [P, MC, HID], t[src].rearrange("(k p) n -> p k n", p=P))
    tile("w3", [P, MC, D], t["w3T"].rearrange("(k p) n -> p k n", p=P))
    for name in ("s1", "s2", "g1", "g2"):
        tile(name, [P, MC], t[name])
    for name, src in (("bias", "out_b"), ("s3", "s3"), ("gamma", "gamma"), ("beta", "beta")):
        tile(name, [P, D], row(src).to_broadcast([P, D]))
    tile("mscale", [P, 1], row("mscale").to_broadcast([P, 1]))
    tile("qk", [P, D], t["qk"])
    tile("ov", [P, D], t["ov"])
    tile("mu", [P, 256], t["mu"].rearrange("d e s -> d (e s)"))
    for name in ("ew1", "ew2"):
        tile(name, [P, 4, P], t[name])
    tile("eb1", [P, 4], t["eb1"])
    for half in range(2):
        tile("eb2", [P, 2, D], t["eb2"][half * 8:half * 8 + 8, :].unsqueeze(1).to_broadcast([8, 16, D]), half)
    return W, loads


def build(nc, t, out):
    def dram(name, shape, dt):
        return nc.dram_tensor(name, shape, dt, kind="Internal").ap()

    q_scr = dram("q_scr", (B, H, NB * HD, S), BF16)
    k_scr = dram("k_scr", (B, H, (NB + 2) * HD, S), BF16)
    v_scr = dram("v_scr", (B, P, NT, D), F32)
    nm_scr = dram("nm_scr", (2, NB * G * QT, P), BF16)
    with ExitStack() as top:
        def sb(ctx, name, shape, dt=F32):
            return ctx.enter_context(nc.sbuf_tensor(name, shape, dt))

        ident, ident16 = sb(top, "ident", [P, P]), sb(top, "ident16", [P, P], BF16)
        ident_done, weights_loaded = (top.enter_context(nc.semaphore(n)) for n in ("ident_done", "weights_loaded"))
        with ExitStack() as ctx:
            make_identity(nc, ctx, ident, ident16, ident_done)
        X = sb(top, "X", [P, TT, D])
        W, loads = weight_tiles(nc, top, t, weights_loaded)
        with ExitStack() as ctx:
            o_raw = sb(ctx, "o_raw", [P, TT, H, HD + 1])
            denom = sb(ctx, "denom", [P, TT * H])
            with ExitStack() as inner:
                in_x = X[:, :, :].rearrange("p t d -> p (t d)").bitcast(BF16).rearrange("p (g h s) -> p g h s", g=NG, h=G)
                q_st = [in_x[:, g, :, :] for g in range(NG)]
                k_st = [sb(inner, f"k_stack{g}", [P, G, S], BF16) for g in range(NG)]
                stack_loaded = [top.enter_context(nc.semaphore(f"stack_loaded{g}")) for g in range(NG)]
                qk_written, v_written = ([top.enter_context(nc.semaphore(f"{n}{i}")) for i in range(2)]
                                         for n in ("qk_written", "v_written"))
                in_o, n_parts = o_raw[:, :, :, :].rearrange("p t h c -> p (t h c)"), 2 * 2 * NB * S // 2
                parts = in_o[:, 0:n_parts].bitcast(BF16).rearrange("p (i o n s) -> p i o n s", i=2, o=2, n=NB)
                v_sb = in_o[:, n_parts:n_parts + 2 * S].rearrange("p (i t d) -> p i t d", i=2, d=D)
                project_qkv(nc, t["xT"], t["wqT"], t["wkT"], t["wvT"], q_scr, k_scr, v_scr, q_st, k_st, stack_loaded,
                            parts, v_sb, qk_written, v_written)
                m_first, m_all = sb(inner, "m_first", [P, TT, H]), sb(inner, "m_all", [P, TT, H])
                head_attention(nc, ident, ident16, q_scr, k_scr, v_scr, nm_scr, q_st, k_st, stack_loaded,
                               parts, v_sb, qk_written, v_written, o_raw, m_first, m_all, loads)
                head_denominators(nc, o_raw, m_first, m_all, denom, weights_loaded, len(loads))
            gated_mlp(nc, ident, t, W, o_raw, denom, X)
        causal_attention(nc, ident, W, X)
        soft_experts(nc, ident, W, X, out)


def kernel(**inputs):
    import numpy as np
    import concourse.bacc as bacc
    from concourse.bass_utils import run_bass_kernel_spmd

    def laid(name):
        return np.ascontiguousarray(inputs[name])

    x = laid("L0_attn_x")
    arrays = {"x": x, "xT": np.ascontiguousarray(x.reshape(B * S, D).T)}
    for name, src in (("wqT", "L0_attn_q_w"), ("wkT", "L0_attn_k_w"), ("wvT", "L0_attn_v_w"), ("woT", "L0_attn_out_w"),
                      ("w1T", "L0_ffn_w1_w"), ("w2T", "L0_ffn_w2_w"), ("h1T", "L0_ffn_h1_w"), ("h2T", "L0_ffn_h2_w"),
                      ("w3T", "L0_ffn_w3_w")):
        arrays[name] = np.ascontiguousarray(laid(src).T)
    for name, src in (("out_b", "L0_attn_out_b"), ("s1", "L0_ffn_w1_s"), ("s2", "L0_ffn_w2_s"), ("g1", "L0_ffn_h1_s"),
                      ("g2", "L0_ffn_h2_s"), ("s3", "L0_ffn_w3_s"), ("qk", "L1_attn_qk"), ("ov", "L1_attn_ov"),
                      ("gamma", "L1_ffn_ln_gamma"), ("beta", "L1_ffn_ln_beta"), ("mu", "L1_ffn_mu"),
                      ("mscale", "L1_ffn_scale"), ("ew1", "L1_ffn_w1"), ("eb1", "L1_ffn_b1"), ("ew2", "L1_ffn_w2"),
                      ("eb2", "L1_ffn_b2")):
        arrays[name] = laid(src)
    for name in ("s1", "s2", "g1", "g2"):
        arrays[name] = np.ascontiguousarray(arrays[name].reshape(MC, P).T)
    arrays["ew1"] = np.ascontiguousarray(arrays["ew1"].reshape(4, 4, D, 32).transpose(2, 0, 1, 3).reshape(D, 4, P))
    arrays["ew2"] = np.ascontiguousarray(arrays["ew2"].reshape(4, P, D).transpose(1, 0, 2))
    arrays["eb1"] = np.ascontiguousarray(arrays["eb1"].reshape(4, P).T)
    nc = bacc.Bacc("TRN2", target_bir_lowering=False, num_devices=1)
    given, fed = {}, {}
    for name, a in arrays.items():
        fed[f"in_{name}"] = a
        given[name] = nc.dram_tensor(f"in_{name}", a.shape, mybir.dt.from_np(a.dtype), kind="ExternalInput").ap()
    out = nc.dram_tensor("out", (B, S, D), F32, kind="ExternalOutput").ap()
    build(nc, given, out)
    return run_bass_kernel_spmd(nc, [fed], core_ids=[0]).results[0]["out"]
```
